# Optimizing a Trainium2 kernel written in Bass

```python
import numpy as np
import jax
import jax.numpy as jnp

def _softmax(x, axis=-1):
    return jax.nn.softmax(x, axis=axis)

def _gelu(x):
    return jax.nn.gelu(x, approximate=True)

def _silu(x):
    return jax.nn.silu(x)

def _sigmoid(x):
    return jax.nn.sigmoid(x)

def _layernorm(x, axis=-1, eps=1e-05):
    m = jnp.mean(x, axis=axis, keepdims=True)
    v = jnp.var(x, axis=axis, keepdims=True)
    return (x - m) / jnp.sqrt(v + eps)

def _scatter_add(tgt, idx, src, axis=0):
    return tgt.at[idx].add(src)

def _segment_sum(src, seg, n):
    return jax.ops.segment_sum(src, seg, n)
kernel_name = 'mk_cond_resid_d4_seqx_r4_5888ce'

def setup_inputs(seed: int=0):
    np.random.seed(seed)
    _w = jnp.asarray

    def _rec_inputs():
        import jax
        import jax.numpy as jnp
        _rk = jax.random.key(seed)
        x = -0.0002928 + 1 * jax.random.normal(jax.random.fold_in(_rk, 1), (2, 1024, 256), jnp.float32)
        _lenS = 1024 - jax.random.randint(jax.random.fold_in(_rk, 7), (2,), 0, max(1, 1024 // 4) + 1, jnp.int32)
        _lenS2 = 1024 - jax.random.randint(jax.random.fold_in(_rk, 8), (2,), 0, max(1, 1024 // 4) + 1, jnp.int32)
        cond_64 = -0.0184271 + 1.00439 * jax.random.normal(jax.random.fold_in(_rk, 12), (2, 64), jnp.float32)
        fside_16xSxS_0 = -5.72187e-05 + 0.999849 * jax.random.normal(jax.random.fold_in(_rk, 13), (16, 1024, 1024), jnp.float32)
        _validS = jnp.arange(1024)[None, :] < _lenS[:, None]
        _validS2 = jnp.arange(1024)[None, :] < _lenS2[:, None]
        _causal = jnp.tril(jnp.ones((1024, 1024), dtype=bool))
        mask_BxS_bf1 = jnp.ones((2, 1024), dtype=bool)
        mask_BxS_bk0 = jnp.logical_not(jnp.broadcast_to(_validS[:, :], (2, 1024)))
        return (x, cond_64, fside_16xSxS_0, mask_BxS_bf1, mask_BxS_bk0)
    x, cond_64, fside_16xSxS_0, mask_BxS_bf1, mask_BxS_bk0 = _rec_inputs()

    def _L0_cond_setup():
        import jax, jax.numpy as jnp
        import numpy as np
        DIM = 256
        HEADS = 16
        DIM_HEAD = 64
        SCALE = 8.0

        def ln(x, g, eps=1e-05):
            mean = x.mean(axis=-1, keepdims=True)
            var = ((x - mean) ** 2).mean(axis=-1, keepdims=True)
            return (x - mean) * jax.lax.rsqrt(var + eps) * g

        def l2norm(t):
            n = jnp.maximum(jnp.linalg.norm(t, axis=-1, keepdims=True), 1e-12)
            return t / n

        def rel_pos_bias(n, w0, b0, g0, w1, b1, g1, w2, b2, dtype):
            pos = jnp.arange(-n + 1, n, dtype=dtype)[:, None]
            h = jax.nn.silu(ln(pos @ w0 + b0, g0))
            h = jax.nn.silu(ln(h @ w1 + b1, g1))
            h = h @ w2 + b2
            i = jnp.arange(n)
            idx = i[:, None] - i[None, :] + n - 1
            bias = h[idx]
            return jnp.transpose(bias, (2, 0, 1))
        key = jax.random.key(seed)
        ks = jax.random.split(key, 16)
        b, n = (2, 512)
        inner = HEADS * DIM_HEAD
        s = 0.02
        return {'x': jax.random.normal(ks[0], (b, n, DIM), jnp.float32), 'mask': jnp.ones((b, n), dtype=bool), 'g_norm': jnp.ones((DIM,), jnp.float32), 'Wq': jax.random.normal(ks[1], (DIM, inner), jnp.float32) * s, 'Wkv': jax.random.normal(ks[2], (DIM, 2 * DIM_HEAD), jnp.float32) * s, 'q_scale': jnp.ones((DIM_HEAD,), jnp.float32), 'k_scale': jnp.ones((DIM_HEAD,), jnp.float32), 'null_kv': jax.random.normal(ks[3], (2, DIM_HEAD), jnp.float32), 'null_attn_bias': jax.random.normal(ks[4], (HEADS,), jnp.float32), 'w0': jax.random.normal(ks[5], (1, DIM), jnp.float32) * s, 'b0': jnp.zeros((DIM,), jnp.float32), 'g0': jnp.ones((DIM,), jnp.float32), 'w1': jax.random.normal(ks[6], (DIM, DIM), jnp.float32) * s, 'b1': jnp.zeros((DIM,), jnp.float32), 'g1': jnp.ones((DIM,), jnp.float32), 'w2': jax.random.normal(ks[7], (DIM, HEADS), jnp.float32) * s, 'b2': jnp.zeros((HEADS,), jnp.float32), 'Wout': jax.random.normal(ks[8], (inner, DIM), jnp.float32) * s, 'g_out': jnp.ones((DIM,), jnp.float32)}
    _L0_cond_all = _L0_cond_setup()
    _L0_cond_in = {k: v for k, v in _L0_cond_all.items() if k in ('g_norm', 'Wq', 'Wkv', 'q_scale', 'k_scale', 'null_attn_bias', 'w0', 'b0', 'g0', 'w1', 'b1', 'g1', 'w2', 'b2', 'Wout', 'g_out')}
    del _L0_cond_all

    def _L1_cond_setup():
        import jax, jax.numpy as jnp
        import numpy as np
        B, S, H = (4, 512, 256)
        E = 8
        M = 128
        K = 2
        N_SHARED = 2
        SM = M * N_SHARED
        G = 64
        GE_TEMP = 1.0
        ALPHA = 0.001
        SEQ_AUX = True
        NORM_TOPK = True
        COS_TEMP = 0.78
        CONS_ALPHA = 0.01
        LEAKY_SLOPE = 0.01
        EPS_COS = 1e-08

        def _leaky(x):
            return jnp.where(x >= 0, x, LEAKY_SLOPE * x)

        def _moe_forward(hidden_states, g, wt, wg, w_gate, w_up, w_down, sw_gate, sw_up, sw_down):
            b, s, h = hidden_states.shape
            x = hidden_states.reshape(-1, h)
            T = x.shape[0]
            logits_h = x @ wt.T
            logits_g = g @ wg.T
            logits_g = jnp.repeat(logits_g, s, axis=0)
            logits = (logits_h + logits_g / GE_TEMP) / (1.0 + 1.0 / GE_TEMP)
            scores = jax.nn.softmax(logits, axis=-1)
            topk_w, topk_idx = jax.lax.top_k(scores, K)
            if K > 1 and NORM_TOPK:
                topk_w = topk_w / (topk_w.sum(-1, keepdims=True) + 1e-20)
            onehot = jax.nn.one_hot(topk_idx.reshape(b, s * K), E, dtype=jnp.float32)
            ce = onehot.sum(1) / (s * K / E)
            aux_loss = (ce * scores.reshape(b, s, E).mean(1)).sum(1).mean() * ALPHA
            gp = _leaky(jnp.einsum('th,ehm->etm', x, w_gate))
            up = jnp.einsum('th,ehm->etm', x, w_up)
            y_all = jnp.einsum('etm,emh->eth', gp * up, w_down)
            y_sel = y_all[topk_idx, jnp.arange(T)[:, None], :]
            y = (y_sel * topk_w[..., None]).sum(1).reshape(b, s, h)
            p = _leaky(hidden_states @ sw_gate) * (hidden_states @ sw_up) @ sw_down
            y = y + p
            num = jnp.sum(y * p, -1)
            den = jnp.maximum(jnp.linalg.norm(y, axis=-1), EPS_COS) * jnp.maximum(jnp.linalg.norm(p, axis=-1), EPS_COS)
            closs = CONS_ALPHA * jnp.mean(num / den / (1.0 + COS_TEMP))
            return (y, aux_loss + closs)
        key = jax.random.key(seed)
        ks = jax.random.split(key, 12)
        sh = 1.0 / np.sqrt(H)
        sm = 1.0 / np.sqrt(M)
        ssm = 1.0 / np.sqrt(SM)
        sg = 1.0 / np.sqrt(G)
        return {'hidden_states': jax.random.normal(ks[0], (B, S, H), jnp.float32), 'g': jax.random.normal(ks[1], (B, G), jnp.float32), 'wt': jax.random.uniform(ks[2], (E, H), jnp.float32, -sh, sh), 'wg': jax.random.uniform(ks[3], (E, G), jnp.float32, -sg, sg), 'w_gate': jax.random.uniform(ks[4], (E, H, M), jnp.float32, -sh, sh), 'w_up': jax.random.uniform(ks[5], (E, H, M), jnp.float32, -sh, sh), 'w_down': jax.random.uniform(ks[6], (E, M, H), jnp.float32, -sm, sm), 'sw_gate': jax.random.uniform(ks[7], (H, SM), jnp.float32, -sh, sh), 'sw_up': jax.random.uniform(ks[8], (H, SM), jnp.float32, -sh, sh), 'sw_down': jax.random.uniform(ks[9], (SM, H), jnp.float32, -ssm, ssm)}
    _L1_cond_all = _L1_cond_setup()
    _L1_cond_in = {k: v for k, v in _L1_cond_all.items() if k in ('wt', 'wg', 'w_gate', 'w_up', 'w_down', 'sw_gate', 'sw_up', 'sw_down')}
    del _L1_cond_all

    def _L2_cond_setup():
        import jax, jax.numpy as jnp
        import numpy as np
        B, N, DIM, H, DH = (2, 512, 256, 16, 64)
        INNER = H * DH
        EPS = 1e-05

        def layernorm(x, g):
            mean = jnp.mean(x, axis=-1, keepdims=True)
            var = jnp.var(x, axis=-1, keepdims=True)
            return (x - mean) * jax.lax.rsqrt(var + EPS) * g
        key = jax.random.key(seed)
        ks = jax.random.split(key, 10)
        x = jax.random.normal(ks[0], (B, N, DIM), dtype=jnp.float32)
        attn_bias = jax.random.normal(ks[1], (H, N, N), dtype=jnp.float32)
        mask = jax.random.randint(ks[2], (B, N), 0, 2).astype(bool)
        g_in = jnp.ones((DIM,), dtype=jnp.float32)
        null_attn_bias = jax.random.normal(ks[3], (H,), dtype=jnp.float32)
        null_kv = jax.random.normal(ks[4], (2, DH), dtype=jnp.float32)
        Wq = jax.random.normal(ks[5], (DIM, INNER), dtype=jnp.float32) * 0.02
        Wkv = jax.random.normal(ks[6], (DIM, 2 * DH), dtype=jnp.float32) * 0.02
        Wo = jax.random.normal(ks[7], (INNER, DIM), dtype=jnp.float32) * 0.02
        g_out = jnp.ones((DIM,), dtype=jnp.float32)
        return {'x': x, 'attn_bias': attn_bias, 'mask': mask, 'g_in': g_in, 'null_attn_bias': null_attn_bias, 'null_kv': null_kv, 'Wq': Wq, 'Wkv': Wkv, 'Wo': Wo, 'g_out': g_out}
    _L2_cond_all = _L2_cond_setup()
    _L2_cond_in = {k: v for k, v in _L2_cond_all.items() if k in ('g_in', 'null_attn_bias', 'Wq', 'Wkv', 'Wo', 'g_out')}
    del _L2_cond_all

    def _L3_cond_setup():
        import jax, jax.numpy as jnp
        import numpy as np
        DIM = 256
        HEADS = 16
        DIM_HEAD = 64
        SCALE = 8.0

        def ln(x, g, eps=1e-05):
            mean = x.mean(axis=-1, keepdims=True)
            var = ((x - mean) ** 2).mean(axis=-1, keepdims=True)
            return (x - mean) * jax.lax.rsqrt(var + eps) * g

        def l2norm(t):
            n = jnp.maximum(jnp.linalg.norm(t, axis=-1, keepdims=True), 1e-12)
            return t / n

        def rel_pos_bias(n, w0, b0, g0, w1, b1, g1, w2, b2, dtype):
            pos = jnp.arange(-n + 1, n, dtype=dtype)[:, None]
            h = jax.nn.silu(ln(pos @ w0 + b0, g0))
            h = jax.nn.silu(ln(h @ w1 + b1, g1))
            h = h @ w2 + b2
            i = jnp.arange(n)
            idx = i[:, None] - i[None, :] + n - 1
            bias = h[idx]
            return jnp.transpose(bias, (2, 0, 1))
        key = jax.random.key(seed)
        ks = jax.random.split(key, 16)
        b, n = (2, 512)
        inner = HEADS * DIM_HEAD
        s = 0.02
        return {'x': jax.random.normal(ks[0], (b, n, DIM), jnp.float32), 'mask': jnp.ones((b, n), dtype=bool), 'g_norm': jnp.ones((DIM,), jnp.float32), 'Wq': jax.random.normal(ks[1], (DIM, inner), jnp.float32) * s, 'Wkv': jax.random.normal(ks[2], (DIM, 2 * DIM_HEAD), jnp.float32) * s, 'q_scale': jnp.ones((DIM_HEAD,), jnp.float32), 'k_scale': jnp.ones((DIM_HEAD,), jnp.float32), 'null_kv': jax.random.normal(ks[3], (2, DIM_HEAD), jnp.float32), 'null_attn_bias': jax.random.normal(ks[4], (HEADS,), jnp.float32), 'w0': jax.random.normal(ks[5], (1, DIM), jnp.float32) * s, 'b0': jnp.zeros((DIM,), jnp.float32), 'g0': jnp.ones((DIM,), jnp.float32), 'w1': jax.random.normal(ks[6], (DIM, DIM), jnp.float32) * s, 'b1': jnp.zeros((DIM,), jnp.float32), 'g1': jnp.ones((DIM,), jnp.float32), 'w2': jax.random.normal(ks[7], (DIM, HEADS), jnp.float32) * s, 'b2': jnp.zeros((HEADS,), jnp.float32), 'Wout': jax.random.normal(ks[8], (inner, DIM), jnp.float32) * s, 'g_out': jnp.ones((DIM,), jnp.float32)}
    _L3_cond_all = _L3_cond_setup()
    _L3_cond_in = {k: v for k, v in _L3_cond_all.items() if k in ('g_norm', 'Wq', 'Wkv', 'q_scale', 'k_scale', 'null_attn_bias', 'w0', 'b0', 'g0', 'w1', 'b1', 'g1', 'w2', 'b2', 'Wout', 'g_out')}
    del _L3_cond_all
    return {'x': x, 'cond_64': cond_64, 'fside_16xSxS_0': fside_16xSxS_0, 'mask_BxS_bf1': mask_BxS_bf1, 'mask_BxS_bk0': mask_BxS_bk0, 'L0_cond_g_norm': _L0_cond_in['g_norm'], 'L0_cond_Wq': _L0_cond_in['Wq'], 'L0_cond_Wkv': _L0_cond_in['Wkv'], 'L0_cond_q_scale': _L0_cond_in['q_scale'], 'L0_cond_k_scale': _L0_cond_in['k_scale'], 'L0_cond_null_attn_bias': _L0_cond_in['null_attn_bias'], 'L0_cond_w0': _L0_cond_in['w0'], 'L0_cond_b0': _L0_cond_in['b0'], 'L0_cond_g0': _L0_cond_in['g0'], 'L0_cond_w1': _L0_cond_in['w1'], 'L0_cond_b1': _L0_cond_in['b1'], 'L0_cond_g1': _L0_cond_in['g1'], 'L0_cond_w2': _L0_cond_in['w2'], 'L0_cond_b2': _L0_cond_in['b2'], 'L0_cond_Wout': _L0_cond_in['Wout'], 'L0_cond_g_out': _L0_cond_in['g_out'], 'L1_cond_wt': _L1_cond_in['wt'], 'L1_cond_wg': _L1_cond_in['wg'], 'L1_cond_w_gate': _L1_cond_in['w_gate'], 'L1_cond_w_up': _L1_cond_in['w_up'], 'L1_cond_w_down': _L1_cond_in['w_down'], 'L1_cond_sw_gate': _L1_cond_in['sw_gate'], 'L1_cond_sw_up': _L1_cond_in['sw_up'], 'L1_cond_sw_down': _L1_cond_in['sw_down'], 'L2_cond_g_in': _L2_cond_in['g_in'], 'L2_cond_null_attn_bias': _L2_cond_in['null_attn_bias'], 'L2_cond_Wq': _L2_cond_in['Wq'], 'L2_cond_Wkv': _L2_cond_in['Wkv'], 'L2_cond_Wo': _L2_cond_in['Wo'], 'L2_cond_g_out': _L2_cond_in['g_out'], 'L3_cond_g_norm': _L3_cond_in['g_norm'], 'L3_cond_Wq': _L3_cond_in['Wq'], 'L3_cond_Wkv': _L3_cond_in['Wkv'], 'L3_cond_q_scale': _L3_cond_in['q_scale'], 'L3_cond_k_scale': _L3_cond_in['k_scale'], 'L3_cond_null_attn_bias': _L3_cond_in['null_attn_bias'], 'L3_cond_w0': _L3_cond_in['w0'], 'L3_cond_b0': _L3_cond_in['b0'], 'L3_cond_g0': _L3_cond_in['g0'], 'L3_cond_w1': _L3_cond_in['w1'], 'L3_cond_b1': _L3_cond_in['b1'], 'L3_cond_g1': _L3_cond_in['g1'], 'L3_cond_w2': _L3_cond_in['w2'], 'L3_cond_b2': _L3_cond_in['b2'], 'L3_cond_Wout': _L3_cond_in['Wout'], 'L3_cond_g_out': _L3_cond_in['g_out']}

def reference(x, cond_64, fside_16xSxS_0, mask_BxS_bf1, mask_BxS_bk0, L0_cond_g_norm, L0_cond_Wq, L0_cond_Wkv, L0_cond_q_scale, L0_cond_k_scale, L0_cond_null_attn_bias, L0_cond_w0, L0_cond_b0, L0_cond_g0, L0_cond_w1, L0_cond_b1, L0_cond_g1, L0_cond_w2, L0_cond_b2, L0_cond_Wout, L0_cond_g_out, L1_cond_wt, L1_cond_wg, L1_cond_w_gate, L1_cond_w_up, L1_cond_w_down, L1_cond_sw_gate, L1_cond_sw_up, L1_cond_sw_down, L2_cond_g_in, L2_cond_null_attn_bias, L2_cond_Wq, L2_cond_Wkv, L2_cond_Wo, L2_cond_g_out, L3_cond_g_norm, L3_cond_Wq, L3_cond_Wkv, L3_cond_q_scale, L3_cond_k_scale, L3_cond_null_attn_bias, L3_cond_w0, L3_cond_b0, L3_cond_g0, L3_cond_w1, L3_cond_b1, L3_cond_g1, L3_cond_w2, L3_cond_b2, L3_cond_Wout, L3_cond_g_out):
    import jax
    import jax.numpy as jnp

    def _L0_cond_ref(x, mask, g_norm, Wq, Wkv, q_scale, k_scale, null_kv, null_attn_bias, w0, b0, g0, w1, b1, g1, w2, b2, Wout, g_out):
        import jax, jax.numpy as jnp
        import numpy as np
        DIM = 256
        HEADS = 16
        DIM_HEAD = 64
        SCALE = 8.0

        def ln(x, g, eps=1e-05):
            mean = x.mean(axis=-1, keepdims=True)
            var = ((x - mean) ** 2).mean(axis=-1, keepdims=True)
            return (x - mean) * jax.lax.rsqrt(var + eps) * g

        def l2norm(t):
            n = jnp.maximum(jnp.linalg.norm(t, axis=-1, keepdims=True), 1e-12)
            return t / n

        def rel_pos_bias(n, w0, b0, g0, w1, b1, g1, w2, b2, dtype):
            pos = jnp.arange(-n + 1, n, dtype=dtype)[:, None]
            h = jax.nn.silu(ln(pos @ w0 + b0, g0))
            h = jax.nn.silu(ln(h @ w1 + b1, g1))
            h = h @ w2 + b2
            i = jnp.arange(n)
            idx = i[:, None] - i[None, :] + n - 1
            bias = h[idx]
            return jnp.transpose(bias, (2, 0, 1))
        b, n, _ = x.shape
        xn = ln(x, g_norm)
        q = (xn @ Wq).reshape(b, n, HEADS, DIM_HEAD).transpose(0, 2, 1, 3)
        kv = xn @ Wkv
        k, v = (kv[..., :DIM_HEAD], kv[..., DIM_HEAD:])
        nk = jnp.broadcast_to(null_kv[0], (b, 1, DIM_HEAD))
        nv = jnp.broadcast_to(null_kv[1], (b, 1, DIM_HEAD))
        k = jnp.concatenate([nk, k], axis=1)
        v = jnp.concatenate([nv, v], axis=1)
        q = l2norm(q) * q_scale
        k = l2norm(k) * k_scale
        sim = jnp.einsum('bhid,bjd->bhij', q, k) * SCALE
        bias = rel_pos_bias(n, w0, b0, g0, w1, b1, g1, w2, b2, q.dtype)
        null_bias = jnp.broadcast_to(null_attn_bias[:, None, None], (HEADS, n, 1))
        attn_bias = jnp.concatenate([null_bias, bias], axis=-1)
        sim = sim + attn_bias
        neg = -jnp.finfo(sim.dtype).max
        causal = jnp.triu(jnp.ones((n, n + 1), dtype=bool), k=2)
        sim = jnp.where(causal, neg, sim)
        m = jnp.pad(mask, ((0, 0), (1, 0)), constant_values=True)[:, None, None, :]
        sim = jnp.where(m, sim, neg)
        attn = jax.nn.softmax(sim, axis=-1)
        out = jnp.einsum('bhij,bjd->bhid', attn, v)
        out = out.transpose(0, 2, 1, 3).reshape(b, n, HEADS * DIM_HEAD)
        return ln(out @ Wout, g_out)

    def _L1_cond_ref(hidden_states, g, wt, wg, w_gate, w_up, w_down, sw_gate, sw_up, sw_down):
        import jax, jax.numpy as jnp
        import numpy as np
        B, S, H = (4, 512, 256)
        E = 8
        M = 128
        K = 2
        N_SHARED = 2
        SM = M * N_SHARED
        G = 64
        GE_TEMP = 1.0
        ALPHA = 0.001
        SEQ_AUX = True
        NORM_TOPK = True
        COS_TEMP = 0.78
        CONS_ALPHA = 0.01
        LEAKY_SLOPE = 0.01
        EPS_COS = 1e-08

        def _leaky(x):
            return jnp.where(x >= 0, x, LEAKY_SLOPE * x)

        def _moe_forward(hidden_states, g, wt, wg, w_gate, w_up, w_down, sw_gate, sw_up, sw_down):
            b, s, h = hidden_states.shape
            x = hidden_states.reshape(-1, h)
            T = x.shape[0]
            logits_h = x @ wt.T
            logits_g = g @ wg.T
            logits_g = jnp.repeat(logits_g, s, axis=0)
            logits = (logits_h + logits_g / GE_TEMP) / (1.0 + 1.0 / GE_TEMP)
            scores = jax.nn.softmax(logits, axis=-1)
            topk_w, topk_idx = jax.lax.top_k(scores, K)
            if K > 1 and NORM_TOPK:
                topk_w = topk_w / (topk_w.sum(-1, keepdims=True) + 1e-20)
            onehot = jax.nn.one_hot(topk_idx.reshape(b, s * K), E, dtype=jnp.float32)
            ce = onehot.sum(1) / (s * K / E)
            aux_loss = (ce * scores.reshape(b, s, E).mean(1)).sum(1).mean() * ALPHA
            gp = _leaky(jnp.einsum('th,ehm->etm', x, w_gate))
            up = jnp.einsum('th,ehm->etm', x, w_up)
            y_all = jnp.einsum('etm,emh->eth', gp * up, w_down)
            y_sel = y_all[topk_idx, jnp.arange(T)[:, None], :]
            y = (y_sel * topk_w[..., None]).sum(1).reshape(b, s, h)
            p = _leaky(hidden_states @ sw_gate) * (hidden_states @ sw_up) @ sw_down
            y = y + p
            num = jnp.sum(y * p, -1)
            den = jnp.maximum(jnp.linalg.norm(y, axis=-1), EPS_COS) * jnp.maximum(jnp.linalg.norm(p, axis=-1), EPS_COS)
            closs = CONS_ALPHA * jnp.mean(num / den / (1.0 + COS_TEMP))
            return (y, aux_loss + closs)
        y, _ = _moe_forward(hidden_states, g, wt, wg, w_gate, w_up, w_down, sw_gate, sw_up, sw_down)
        return y

    def _L2_cond_ref(x, attn_bias, mask, g_in, null_attn_bias, null_kv, Wq, Wkv, Wo, g_out):
        import jax, jax.numpy as jnp
        import numpy as np
        B, N, DIM, H, DH = (2, 512, 256, 16, 64)
        INNER = H * DH
        EPS = 1e-05

        def layernorm(x, g):
            mean = jnp.mean(x, axis=-1, keepdims=True)
            var = jnp.var(x, axis=-1, keepdims=True)
            return (x - mean) * jax.lax.rsqrt(var + EPS) * g
        b, n, _ = x.shape
        scale = DH ** (-0.5)
        xn = layernorm(x, g_in)
        q = (xn @ Wq).reshape(b, n, H, DH).transpose(0, 2, 1, 3) * scale
        kv = xn @ Wkv
        k, v = (kv[..., :DH], kv[..., DH:])
        nk = jnp.broadcast_to(null_kv[0], (b, 1, DH))
        nv = jnp.broadcast_to(null_kv[1], (b, 1, DH))
        k = jnp.concatenate([nk, k], axis=1)
        v = jnp.concatenate([nv, v], axis=1)
        sim = jnp.einsum('bhid,bjd->bhij', q, k)
        null_col = jnp.broadcast_to(null_attn_bias[:, None, None], (H, n, 1))
        bias = jnp.concatenate([null_col, attn_bias], axis=-1)
        sim = sim + bias
        neg = -jnp.finfo(sim.dtype).max
        j = n + 1
        causal_mask = jnp.triu(jnp.ones((n, j), dtype=bool), k=j - n + 1)
        sim = jnp.where(causal_mask, neg, sim)
        mask_p = jnp.pad(mask, ((0, 0), (1, 0)), constant_values=True)
        sim = jnp.where(mask_p[:, None, None, :], sim, neg)
        attn = jax.nn.softmax(sim, axis=-1)
        out = jnp.einsum('bhij,bjd->bhid', attn, v)
        out = out.transpose(0, 2, 1, 3).reshape(b, n, INNER)
        out = out @ Wo
        return layernorm(out, g_out)

    def _L3_cond_ref(x, mask, g_norm, Wq, Wkv, q_scale, k_scale, null_kv, null_attn_bias, w0, b0, g0, w1, b1, g1, w2, b2, Wout, g_out):
        import jax, jax.numpy as jnp
        import numpy as np
        DIM = 256
        HEADS = 16
        DIM_HEAD = 64
        SCALE = 8.0

        def ln(x, g, eps=1e-05):
            mean = x.mean(axis=-1, keepdims=True)
            var = ((x - mean) ** 2).mean(axis=-1, keepdims=True)
            return (x - mean) * jax.lax.rsqrt(var + eps) * g

        def l2norm(t):
            n = jnp.maximum(jnp.linalg.norm(t, axis=-1, keepdims=True), 1e-12)
            return t / n

        def rel_pos_bias(n, w0, b0, g0, w1, b1, g1, w2, b2, dtype):
            pos = jnp.arange(-n + 1, n, dtype=dtype)[:, None]
            h = jax.nn.silu(ln(pos @ w0 + b0, g0))
            h = jax.nn.silu(ln(h @ w1 + b1, g1))
            h = h @ w2 + b2
            i = jnp.arange(n)
            idx = i[:, None] - i[None, :] + n - 1
            bias = h[idx]
            return jnp.transpose(bias, (2, 0, 1))
        b, n, _ = x.shape
        xn = ln(x, g_norm)
        q = (xn @ Wq).reshape(b, n, HEADS, DIM_HEAD).transpose(0, 2, 1, 3)
        kv = xn @ Wkv
        k, v = (kv[..., :DIM_HEAD], kv[..., DIM_HEAD:])
        nk = jnp.broadcast_to(null_kv[0], (b, 1, DIM_HEAD))
        nv = jnp.broadcast_to(null_kv[1], (b, 1, DIM_HEAD))
        k = jnp.concatenate([nk, k], axis=1)
        v = jnp.concatenate([nv, v], axis=1)
        q = l2norm(q) * q_scale
        k = l2norm(k) * k_scale
        sim = jnp.einsum('bhid,bjd->bhij', q, k) * SCALE
        bias = rel_pos_bias(n, w0, b0, g0, w1, b1, g1, w2, b2, q.dtype)
        null_bias = jnp.broadcast_to(null_attn_bias[:, None, None], (HEADS, n, 1))
        attn_bias = jnp.concatenate([null_bias, bias], axis=-1)
        sim = sim + attn_bias
        neg = -jnp.finfo(sim.dtype).max
        causal = jnp.triu(jnp.ones((n, n + 1), dtype=bool), k=2)
        sim = jnp.where(causal, neg, sim)
        m = jnp.pad(mask, ((0, 0), (1, 0)), constant_values=True)[:, None, None, :]
        sim = jnp.where(m, sim, neg)
        attn = jax.nn.softmax(sim, axis=-1)
        out = jnp.einsum('bhij,bjd->bhid', attn, v)
        out = out.transpose(0, 2, 1, 3).reshape(b, n, HEADS * DIM_HEAD)
        return ln(out @ Wout, g_out)
    x = x + _L0_cond_ref(x, mask_BxS_bf1, L0_cond_g_norm, L0_cond_Wq, L0_cond_Wkv, L0_cond_q_scale, L0_cond_k_scale, cond_64, L0_cond_null_attn_bias, L0_cond_w0, L0_cond_b0, L0_cond_g0, L0_cond_w1, L0_cond_b1, L0_cond_g1, L0_cond_w2, L0_cond_b2, L0_cond_Wout, L0_cond_g_out)
    x = x + _L1_cond_ref(x, cond_64, L1_cond_wt, L1_cond_wg, L1_cond_w_gate, L1_cond_w_up, L1_cond_w_down, L1_cond_sw_gate, L1_cond_sw_up, L1_cond_sw_down)
    x = x + _L2_cond_ref(x, fside_16xSxS_0, mask_BxS_bk0, L2_cond_g_in, L2_cond_null_attn_bias, cond_64, L2_cond_Wq, L2_cond_Wkv, L2_cond_Wo, L2_cond_g_out)
    x = x + _L3_cond_ref(x, mask_BxS_bf1, L3_cond_g_norm, L3_cond_Wq, L3_cond_Wkv, L3_cond_q_scale, L3_cond_k_scale, cond_64, L3_cond_null_attn_bias, L3_cond_w0, L3_cond_b0, L3_cond_g0, L3_cond_w1, L3_cond_b1, L3_cond_g1, L3_cond_w2, L3_cond_b2, L3_cond_Wout, L3_cond_g_out)
    return x

_drawn_inputs = setup_inputs


def setup_inputs(seed=0):
    import zlib

    import numpy as np

    out = dict(_drawn_inputs(seed))
    spreads = {'L0_cond_g_norm': (1.0, 0.2),
     'L0_cond_q_scale': (1.0, 0.2),
     'L0_cond_k_scale': (1.0, 0.2),
     'L0_cond_b0': (0.0, 0.489),
     'L0_cond_g0': (1.0, 0.6),
     'L0_cond_b1': (0.0, 0.517),
     'L0_cond_g1': (1.0, 0.6),
     'L0_cond_b2': (0.0, 0.63),
     'L0_cond_g_out': (1.0, 0.2),
     'L2_cond_g_in': (1.0, 0.2),
     'L2_cond_g_out': (1.0, 0.2),
     'L3_cond_g_norm': (1.0, 0.2),
     'L3_cond_q_scale': (1.0, 0.6),
     'L3_cond_k_scale': (1.0, 0.6),
     'L3_cond_b0': (0.0, 0.8),
     'L3_cond_g0': (1.0, 0.6),
     'L3_cond_b1': (0.0, 0.8),
     'L3_cond_g1': (1.0, 0.6),
     'L3_cond_b2': (0.0, 0.8),
     'L3_cond_g_out': (1.0, 0.2)}
    factors = {'L2_cond_Wq': 3.696, 'L3_cond_w0': 6.564, 'L3_cond_w1': 5.869, 'L3_cond_w2': 6.371}
    for name, (base, spread) in spreads.items():
        noise = np.random.default_rng([zlib.crc32(name.encode()), seed]).standard_normal(out[name].shape)
        drawn = base * np.exp(spread * noise) if base else spread * noise
        out[name] = jnp.asarray(drawn.astype(out[name].dtype))
    for name, factor in factors.items():
        out[name] = (out[name] * factor).astype(out[name].dtype)
    return out
```

```python
from contextlib import ExitStack

import numpy as np
import concourse.bass as bass
from concourse import mybir

F32 = mybir.dt.float32
F32R = mybir.dt.float32r
F16 = mybir.dt.float16
I32 = mybir.dt.int32
U32 = mybir.dt.uint32
U8 = mybir.dt.uint8
ALU = mybir.AluOpType
ACT = mybir.ActivationFunctionType
AX_X = mybir.AxisListType.X
AX_XY = mybir.AxisListType.XY

P = 128
B, S, D = 2, 1024, 256
H, DH = 16, 64
KD = D // P
NT = B * S // P
RT = S // P
TRI = RT * (RT + 1) // 2
GROUPS = TRI // 4
E, M = 8, 128
BIG = float(2 ** 100)
EPS = 1e-5
PITCH = S + P
ONE_BANK = 512
P_SCALE = float(2 ** 15)
V_SCALE = float(2 ** 14)


def wait(eng, sem, value):
    if isinstance(value, int) and value <= 0:
        return
    eng.wait_ge(sem, value)


def wait_alone(eng, sem, value):
    if isinstance(value, int):
        if value > 0:
            eng.wait_ge(sem, value)
        return
    eng.wait_ge(sem, value)
    eng.nop(nofuse=True)


def row_of(ap, n, parts=P):
    return bass.AP(tensor=ap.tensor, offset=ap.offset, ap=[[0, parts], [1, n]])


def spread(ap, n):
    return ap.unsqueeze(2).to_broadcast([ap.shape[0], ap.shape[1], n])


def repeat(ap, n):
    return ap.unsqueeze(1).to_broadcast([ap.shape[0], n, ap.shape[1]])


def very_first(u):
    return isinstance(u[0], int) and u[0] == 0 and u[1] == 0


class Scope:

    def __init__(self, nc, tag):
        self.nc, self.tag, self.ctx, self.sems = nc, tag, ExitStack(), []

    def sb(self, name, shape, dt=F32):
        return self.ctx.enter_context(self.nc.sbuf_tensor(f"{self.tag}_{name}", shape, dt))

    def ps(self, name, shape, dt=F32):
        return self.ctx.enter_context(self.nc.psum_tensor(f"{self.tag}_{name}", shape, dt))

    def sem(self, name):
        s = self.ctx.enter_context(self.nc.semaphore(f"{self.tag}_{name}"))
        self.sems.append(s)
        return s

    def close(self):
        nums = [s.num for s in self.sems]
        self.nc.all_engine_barrier(sems_to_clear=range(min(nums), max(nums) + 1))
        self.ctx.close()


def in_pairs(eng, pairs, body):
    body(0, False)
    with eng.Fori(1, pairs - 1) as i:
        body(i, False)
    body(pairs - 1, True)


def pipelined(eng, tiles, plan):
    first = max(0, -min(ahead for _, ahead in plan))
    deep = max(0, max(ahead for _, ahead in plan))

    def step(i, off):
        for stage, ahead in plan:
            if not isinstance(i, int):
                stage((i, off + ahead))
            elif 0 <= off + ahead < tiles:
                stage((0, off + ahead))
    begin = (first + 3) // 2
    end = (tiles - deep) // 2
    for t in range(-deep, 2 * begin):
        step(0, t)
    with eng.Fori(begin, end) as i:
        step(i, 0)
        step(i, 1)
    for t in range(2 * end, tiles + first):
        step(0, t)


def of(t, n, c=0):
    i, off = t
    return i * (2 * n) + (off * n + c)


def at(t, width=1):
    i, off = t
    if isinstance(i, int):
        return slice((2 * i + off) * width, (2 * i + off + 1) * width)
    return bass.ds(of(t, width), width)


def bias_tables(nc, keep, tag, w0, b0, g0, w1, b1, g1, w2, b2, shifted):
    sc = Scope(nc, tag)
    sb, ps, sem = sc.sb, sc.ps, sc.sem
    NP = S // P
    w0r, b0r, g0r, b1r, g1r = (sb(n, [P, D]) for n in ("w0r", "b0r", "g0r", "b1r", "g1r"))
    w1s = sb("w1s", [P, KD, D])
    w2s = sb("w2s", [P, KD, H])
    b2c = sb("b2c", [H, 1])
    dist_i = sb("dist_i", [P, NP], I32)
    dist = sb("dist", [P, NP])
    h0 = sb("h0", [P, NP, D])
    h1 = sb("h1", [P, NP, D])
    stat = sb("stat", [P, NP, 6])
    mv = sb("mv", [P, NP, 2])
    std = sb("std", [P, NP])
    rstd = sb("rstd", [P, NP])
    hT = sb("hT", [P, KD, S])
    table = sb("table", [H, PITCH])
    t_ps = ps("t_ps", [P, 2, ONE_BANK])
    m_ps = ps("m_ps", [P, 2, ONE_BANK])
    b_ps = ps("b_ps", [H, S])
    loaded, dist_made, dve, std_made, h_made = (
        sem(n) for n in ("loaded", "dist_made", "dve", "std_made", "h_made"))
    turned, taken, product, tab, stored = (sem(n) for n in ("turned", "taken", "product", "tab", "stored"))
    eps_made = sem("eps_made")
    eps = sb("eps", [P, 1])
    ident = keep["ident"]
    mark = {}

    with nc.Block() as block:
        @block.sync
        def _(sp):
            loads = [(w0r, row_of(w0, D)), (b0r, row_of(b0, D)), (g0r, row_of(g0, D)),
                     (b1r, row_of(b1, D)), (g1r, row_of(g1, D))]
            for dst, src in loads:
                sp.dma_start(dst[:, :], src).then_inc(loaded, 16)
            sp.dma_start(w1s[:, :, :], w1.rearrange("(k p) n -> p k n", p=P)).then_inc(loaded, 16)
            sp.dma_start(w2s[:, :, :], w2.rearrange("(k p) n -> p k n", p=P)).then_inc(loaded, 16)
            sp.dma_start(b2c[:, :], b2.rearrange("(h a) -> h a", a=1)).then_inc(loaded, 16)
            sp.wait_ge(tab, 4)
            for h in range(H):
                src = table[h:h + 1, 0:PITCH - 1].unsqueeze(1).to_broadcast([1, P, PITCH - 1])
                dst = bass.AP(tensor=shifted.tensor, offset=shifted.offset + h * (P + 1) * PITCH,
                              ap=[[1, 1], [PITCH + 1, P], [1, PITCH - 1]])
                sp.dma_start(dst, src).then_inc(stored, 16)
            sp.wait_ge(stored, 16 * H)

        @block.gpsimd
        def _(pool):
            pool.iota(dist_i[:, :], [[-P, NP]], base=S - 1, channel_multiplier=-1).then_inc(dist_made, 1)

        @block.vector
        def _(v):
            done = [0]

            def link(ins):
                done[0] += 1
                ins.then_inc(dve, 1)
                v.wait_ge(dve, done[0])

            def norm(src, dst, gain, which):
                for q in range(NP):
                    last = v.bn_stats(stat[:, q, :], src[:, q, :])
                link(last)
                for q in range(NP):
                    last = v.bn_aggr(mv[:, q, :], stat[:, q, :])
                link(last)
                mark[which, "var"] = done[0]
                v.wait_ge(std_made, which + 1)
                link(v.reciprocal(rstd[:, :], std[:, :]))
                for q in range(NP):
                    last = v.tensor_scalar(src[:, q, :], src[:, q, :], mv[:, q, 0:1], rstd[:, q:q + 1],
                                           ALU.subtract, ALU.mult)
                link(last)
                link(v.tensor_tensor(dst[:, :, :], src[:, :, :], repeat(gain[:, :], NP), ALU.mult))
                mark[which, "norm"] = done[0]

            v.memset(eps[:, :], EPS).then_inc(eps_made, 1)
            v.memset(table[:, S:PITCH], BIG).then_inc(tab, 1)
            v.wait_ge(dist_made, 1)
            v.wait_ge(loaded, 16 * 8)
            link(v.tensor_copy(dist[:, :], dist_i[:, :]))
            for q in range(NP):
                last = v.scalar_tensor_tensor(out=h0[:, q, :], in0=w0r[:, :], scalar=dist[:, q:q + 1],
                                              in1=b0r[:, :], op0=ALU.mult, op1=ALU.add)
            link(last)
            norm(h0, h1, g0r, 0)
            for q in range(NP):
                v.wait_ge(product, q + 1)
                last = v.tensor_tensor(h0[:, q, :], m_ps[:, q % 2, 0:D], b1r[:, :], ALU.add)
                last.then_inc(dve, 1)
                done[0] += 1
            v.wait_ge(dve, done[0])
            mark["h1"] = done[0]
            norm(h0, h1, g1r, 1)
            for c in range(2):
                v.wait_ge(product, NP + c + 1)
                v.tensor_scalar(table[:, c * ONE_BANK:(c + 1) * ONE_BANK],
                                b_ps[:, c * ONE_BANK:(c + 1) * ONE_BANK], b2c[:, :], -1.0,
                                ALU.add, ALU.mult).then_inc(tab, 1)
            v.sem_inc(tab, 1)

        @block.scalar
        def _(a):
            a.wait_ge(eps_made, 1)
            for which in range(2):
                a.wait_ge(dve, mark[which, "var"])
                a.activation(std[:, :], mv[:, :, 1], ACT.Sqrt, bias=eps[:, :]).then_inc(std_made, 1)
                a.wait_ge(dve, mark[which, "norm"])
                a.activation(h1[:, :, :], h1[:, :, :], ACT.Silu).then_inc(h_made, 1)
                for q in range(NP):
                    a.wait_ge(turned, which * NP + q + 1)
                    if which and q == 0:
                        a.wait_ge(product, NP)
                    a.activation(hT[:, :, q * P:(q + 1) * P],
                                 t_ps[:, q % 2, 0:KD * P].rearrange("p (k n) -> p k n", k=KD),
                                 ACT.Copy).then_inc(taken, 1)

        @block.tensor
        def _(pe):
            pe.wait_ge(loaded, 16 * 8)
            for which in range(2):
                pe.wait_ge(h_made, which + 1)
                for q in range(NP):
                    n = which * NP + q
                    wait(pe, taken, n - 1)
                    for k in range(KD):
                        last = pe.transpose(t_ps[:, q % 2, k * P:(k + 1) * P],
                                            h1[:, q, k * P:(k + 1) * P], ident[:, :])
                    last.then_inc(turned, 1)
                    if which == 0:
                        pe.wait_ge(taken, n + 1)
                        if q >= 2:
                            pe.wait_ge(dve, mark["h1"] - NP + q - 1)
                        for k in range(KD):
                            last = pe.matmul(m_ps[:, q % 2, 0:D], hT[:, k, q * P:(q + 1) * P],
                                             w1s[:, k, :], start=k == 0, stop=k == KD - 1)
                        last.then_inc(product, 1)
            pe.wait_ge(taken, 2 * NP)
            for c in range(2):
                for k in range(KD):
                    last = pe.matmul(b_ps[:, c * ONE_BANK:(c + 1) * ONE_BANK], w2s[:, k, :],
                                     hT[:, k, c * ONE_BANK:(c + 1) * ONE_BANK],
                                     start=k == 0, stop=k == KD - 1)
                last.then_inc(product, 1)
    sc.close()


def project(nc, keep, tag, cosine, Wq, Wkv, g_in, q_scale, k_scale, null_bias, cond, mask, qT_dram, wait_tables=None):
    sc = Scope(nc, tag)
    sb, ps, sem = sc.sb, sc.ps, sc.sem
    ident, X, K1, K2, V, NS = (keep[n] for n in ("ident", "X", "K1", "K2", "V", "NS"))
    v_raw = sb("v_raw", [P, NT, DH])
    v_scaled = sb("v_scaled", [P, NT, DH])
    vmx = sb("vmx", [P, 4])
    vrow = sb("vrow", [1, P])
    vtop = sb("vtop", [1, 2])
    ones = sb("ones", [1, P])
    sign = -1.0 if cosine else 1.0
    factor = -8.0 if cosine else DH ** -0.5
    HK = H + 1
    W = sb("W", [P, KD, H * DH])
    Wk = sb("Wk", [P, KD, 2 * DH])
    gcol = sb("gcol", [P, KD])
    qsr, ksr = sb("qsr", [P, DH]), sb("ksr", [P, DH])
    kf = sb("kf", [P, DH])
    nk = sb("nk", [P, DH])
    nksq = sb("nksq", [P, DH])
    nks = sb("nks", [P, 4])
    nkf = sb("nkf", [P, DH])
    nb = sb("nb", [P, H])
    mask8 = sb("mask8", [P, NT], U8)
    maskf = sb("maskf", [P, NT])
    eps = sb("eps", [P, 1])
    stat = sb("stat", [P, NT, 6])
    mv = sb("mv", [P, NT, 2])
    std = sb("std", [P, NT])
    rstd = sb("rstd", [P, NT])
    xn = sb("xn", [P, 2, D])
    xT = sb("xT", [P, 2, KD, P])
    qs = sb("qs", [P, 2, HK, DH])
    sq = sb("sq", [P, HK, DH])
    ss = sb("ss", [P, HK])
    nrm = sb("nrm", [P, HK])
    rn = sb("rn", [P, HK])
    qn = sb("qn", [P, 2, HK, DH]) if cosine else qs
    kn = sb("kn", [P, 2, DH])
    nprod = sb("nprod", [P, 2, H, DH])
    nsum = sb("nsum", [P, H])
    QR = sb("QR", [P, 2, H + 2, P], F32R)
    QRf = QR[:, :, :, :].bitcast(F32)
    qTs = sb("qTs", [P, 2, H, P])
    x_ps = ps("x_ps", [P, ONE_BANK])
    q_ps = ps("q_ps", [P, H * DH])
    kv_ps = ps("kv_ps", [P, ONE_BANK])
    tr_ps = ps("tr_ps", [P, 2, ONE_BANK])
    (params, w_ready, var_ready, std_ready, null_sq, null_std, dve0, eps_ready, rstd_ready) = (
        sem(n) for n in ("params", "w_ready", "var_ready", "std_ready", "null_sq", "null_std", "dve0",
                         "eps_ready", "rstd_ready"))
    (xn_ready, x_turned, xT_ready, q_product, q_taken, sq_ready, ss_ready, nrm_ready, qn_ready,
     kn_ready, null_prod, q_hi, k_hi, q_lo, null_sum, null_done, chain) = (
        sem(n) for n in ("xn_ready", "x_turned", "xT_ready", "q_product", "q_taken",
                         "sq_ready", "ss_ready", "nrm_ready", "qn_ready", "kn_ready", "null_prod",
                         "q_hi", "k_hi", "q_lo", "null_sum", "null_done", "chain"))
    turned = [sem("turned0"), sem("turned1")]
    emptied = [sem("emptied0"), sem("emptied1")]
    v_max, v_turned, v_top, v_spread, v_scaling, v_hi = (
        sem(n) for n in ("v_max", "v_turned", "v_top", "v_spread", "v_scaling", "v_hi"))
    q_stored = [sem("q_stored0"), sem("q_stored1")]
    NPARAM = 9 if cosine else 7
    per = [3, 2]

    with nc.Block() as block:
        @block.sync
        def _(sp):
            sp.dma_start(W[:, :, :], Wq.rearrange("(k p) n -> p k n", p=P)).then_inc(params, 16)
            sp.dma_start(Wk[:, :, :], Wkv.rearrange("(k p) n -> p k n", p=P)).then_inc(params, 16)
            sp.dma_start(gcol[:, :], g_in.rearrange("(k p) -> p k", p=P),
                         allow_slow_non_contiguous=True).then_inc(params, 16)
            sp.dma_start(nk[:, :], row_of(cond, DH)).then_inc(params, 16)
            sp.dma_start(keep["NV"][:, :], row_of(cond[1:2, :], DH)).then_inc(params, 16)
            sp.dma_start(nb[:, :], row_of(null_bias, H)).then_inc(params, 16)
            sp.dma_start(mask8[:, :].rearrange("p (b t) -> p b t", b=B),
                         mask.rearrange("b (t p) -> p b t", p=P),
                         allow_slow_non_contiguous=True).then_inc(params, 16)
            if cosine:
                sp.dma_start(qsr[:, :], row_of(q_scale, DH)).then_inc(params, 16)
                sp.dma_start(ksr[:, :], row_of(k_scale, DH)).then_inc(params, 16)

            def store(t):
                par = t[1] % 2
                wait_alone(sp, emptied[0], of(t, per[0], 2))
                wait_alone(sp, emptied[1], of(t, per[1], 2))
                sp.dma_start(qT_dram[:, :, at(t, P)].rearrange("h p n -> p h n"),
                             qTs[:, par, :, :]).then_inc(q_stored[par], 16)
            pipelined(sp, NT, [(store, 0)])
            if wait_tables is not None:
                sp.wait_ge(wait_tables, 16 * H)
            for off in range(2):
                sp.wait_ge(q_stored[off], 16 * (NT // 2))

        @block.gpsimd
        def _(pool):
            pool.wait_ge(w_ready, 1)

            def null_and_k(t):
                par = t[1] % 2
                wait(pool, qn_ready if cosine else q_taken, of(t, 1, 1))
                wait(pool, q_lo, of(t, 1, -1))
                pool.tensor_tensor(kn[:, par, :], qn[:, par, H, :], kf[:, :], ALU.mult).then_inc(kn_ready, 1)
                wait(pool, null_done, of(t, 1, -1))
                pool.tensor_tensor(nprod[:, par, :, :], qn[:, par, 0:H, :], repeat(nkf[:, :], H),
                                   ALU.mult).then_inc(null_prod, 1)
            pipelined(pool, NT, [(null_and_k, 1)])

        @block.vector
        def _(v):
            done = [0]

            def link(ins):
                done[0] += 1
                ins.then_inc(dve0, 1)
                v.wait_ge(dve0, done[0])

            v.memset(eps[:, :], EPS).then_inc(eps_ready, 1)
            for t in range(NT):
                last = v.bn_stats(stat[:, t, :], X[:, t, :])
            link(last)
            for t in range(NT):
                last = v.bn_aggr(mv[:, t, :], stat[:, t, :])
            last.then_inc(var_ready, 1)
            v.wait_ge(params, 16 * NPARAM)
            if cosine:
                link(v.tensor_tensor(nksq[:, :], nk[:, :], nk[:, :], ALU.mult))
                v.tensor_reduce(nks[:, 0:1], nksq[:, :], AX_X, ALU.add).then_inc(null_sq, 1)
                link(v.tensor_tensor(kf[:, :], qsr[:, :], ksr[:, :], ALU.mult))
                link(v.tensor_scalar(kf[:, :], kf[:, :], factor, None, ALU.mult))
            else:
                link(v.memset(kf[:, :], factor))
            for k in range(KD):
                v.tensor_scalar(W[:, k, :], W[:, k, :], gcol[:, k:k + 1], None, ALU.mult)
                last = v.tensor_scalar(Wk[:, k, :], Wk[:, k, :], gcol[:, k:k + 1], None, ALU.mult)
            link(last)
            link(v.tensor_scalar(nb[:, :], nb[:, :], sign, None, ALU.mult))
            link(v.tensor_copy(maskf[:, :], mask8[:, :]))
            link(v.tensor_scalar(maskf[:, :], maskf[:, :], sign * BIG, -sign * BIG, ALU.mult, ALU.add))
            if cosine:
                v.wait_ge(null_std, 1)
                link(v.tensor_scalar(nks[:, 2:3], nks[:, 1:2], 1e-12, None, ALU.max))
                link(v.reciprocal(nks[:, 3:4], nks[:, 2:3]))
                link(v.tensor_scalar(nksq[:, :], nk[:, :], nks[:, 3:4], None, ALU.mult))
                v.tensor_tensor(nkf[:, :], nksq[:, :], kf[:, :], ALU.mult).then_inc(w_ready, 1)
            else:
                v.tensor_tensor(nkf[:, :], nk[:, :], kf[:, :], ALU.mult).then_inc(w_ready, 1)
            v.wait_ge(std_ready, 1)
            v.reciprocal(rstd[:, :], std[:, :]).then_inc(rstd_ready, 1)
            v.wait_ge(rstd_ready, 1)

            def normalise(t):
                par = t[1] % 2
                wait(v, x_turned, of(t, 1, -1))
                v.tensor_scalar(xn[:, par, :], X[:, at(t), :].rearrange("p a n -> p (a n)"), mv[:, at(t), 0],
                                rstd[:, at(t)], ALU.subtract, ALU.mult).then_inc(xn_ready, 1)

            def norms(t):
                wait(v, sq_ready, of(t, 1, 1))
                v.tensor_reduce(ss[:, :], sq[:, :, :], AX_X, ALU.add).then_inc(ss_ready, 1)

            def scale(t):
                par = t[1] % 2
                wait(v, nrm_ready, of(t, 1, 1))
                v.tensor_scalar(rn[:, :], nrm[:, :], 1e-12, None, ALU.max).then_inc(chain, 1)
                wait(v, chain, of(t, 2, 1))
                v.reciprocal(rn[:, :], rn[:, :]).then_inc(chain, 1)
                wait(v, chain, of(t, 2, 2))
                wait(v, k_hi, of(t, 1, -1))
                wait(v, null_prod, of(t, 1, -1))
                v.tensor_tensor(qn[:, par, :, :], qs[:, par, :, :], spread(rn[:, :], DH),
                                ALU.mult).then_inc(qn_ready, 1)

            def low_halves(t):
                par = t[1] % 2
                wait(v, q_hi, of(t, 1, 1))
                v.tensor_tensor(QR[:, par, 0:H, DH:P], qn[:, par, 0:H, :], QRf[:, par, 0:H, 0:DH], ALU.subtract)
                v.tensor_copy(QR[:, par, H + 1, DH:DH + 1], maskf[:, at(t)])
                wait(v, k_hi, of(t, 1, 1))
                v.tensor_tensor(QR[:, par, H + 1, 0:DH], kn[:, par, :], QRf[:, par, H, 0:DH],
                                ALU.subtract).then_inc(q_lo, 1)

            def empty(t, j):
                par, g = t[1] % 2, 2 * j + 1
                wait(v, turned[1], of(t, per[1], j + 1))
                if j == 0:
                    wait(v, q_stored[par], t[0] * 16 + t[1] // 2 * 16)
                v.tensor_copy(qTs[:, par, 4 * g:4 * g + 4, :],
                              tr_ps[:, 1, :].rearrange("p (a n) -> p a n", a=4)).then_inc(emptied[1], 1)

            def null_scores(t):
                wait(v, null_prod, of(t, 1, 1))
                v.tensor_reduce(nsum[:, :], nprod[:, t[1] % 2, :, :], AX_X, ALU.add).then_inc(null_sum, 1)
                wait(v, null_sum, of(t, 1, 1))
                v.tensor_tensor(NS[:, :, at(t)], nsum[:, :].unsqueeze(2), nb[:, :].unsqueeze(2),
                                ALU.add).then_inc(null_done, 1)

            head = [(normalise, 3), (low_halves, 0)]
            tail = [(lambda t: empty(t, 0), 0), (null_scores, 0), (lambda t: empty(t, 1), 0)]
            pipelined(v, NT, head + [(norms, 1)] + tail + [(scale, 1)] if cosine else head + tail)
            v.wait_ge(q_taken, NT)
            link(v.tensor_reduce(vmx[:, 0:1], v_raw[:, :, :], AX_XY, ALU.max))
            link(v.tensor_reduce(vmx[:, 1:2], v_raw[:, :, :], AX_XY, ALU.min))
            link(v.tensor_scalar(vmx[:, 2:3], vmx[:, 1:2], -1.0, None, ALU.mult))
            v.tensor_tensor(vmx[:, 3:4], vmx[:, 0:1], vmx[:, 2:3], ALU.max).then_inc(v_max, 1)
            v.memset(ones[:, :], 1.0).then_inc(v_max, 1)
            v.wait_ge(v_turned, 1)
            link(v.tensor_reduce(vtop[:, 0:1], x_ps[0:1, 0:P], AX_X, ALU.max))
            v.tensor_scalar(vtop[:, 1:2], vtop[:, 0:1], 1e-30, None, ALU.max).then_inc(v_top, 1)
            v.wait_ge(v_spread, 1)
            link(v.tensor_scalar(keep["v_back"][:, :], x_ps[:, P:P + 1], 1.0 / (P_SCALE * V_SCALE), None, ALU.mult))
            link(v.reciprocal(vmx[:, 0:1], x_ps[:, P:P + 1]))
            link(v.tensor_scalar(v_scaled[:, :, :], v_raw[:, :, :], vmx[:, 0:1], V_SCALE, ALU.mult, ALU.mult))
            link(v.tensor_copy(V[:, :, 0:DH], v_scaled[:, :, :]))
            v.tensor_tensor(V[:, :, DH:2 * DH], v_scaled[:, :, :], V[:, :, 0:DH], ALU.subtract).then_inc(v_hi, 1)

        @block.scalar
        def _(a):
            a.wait_ge(eps_ready, 1)
            a.wait_ge(var_ready, 1)
            a.activation(std[:, :], mv[:, :, 1], ACT.Sqrt, bias=eps[:, :]).then_inc(std_ready, 1)
            if cosine:
                a.wait_ge(null_sq, 1)
                a.activation(nks[:, 1:2], nks[:, 0:1], ACT.Sqrt).then_inc(null_std, 1)

            def take_x(t):
                wait(a, x_turned, of(t, 1, 1))
                wait(a, q_product, of(t, 1, -1))
                a.activation(xT[:, t[1] % 2, :, :], x_ps[:, 0:KD * P].rearrange("p (k n) -> p k n", k=KD),
                             ACT.Copy).then_inc(xT_ready, 1)

            def take_qkv(t):
                par = t[1] % 2
                wait(a, q_product, of(t, 1, 1))
                if cosine:
                    wait(a, qn_ready, of(t, 1, -1))
                else:
                    wait(a, q_lo, of(t, 1, -1))
                    wait(a, null_prod, of(t, 1, -1))
                a.activation(qs[:, par, 0:H, :], q_ps[:, :].rearrange("p (h n) -> p h n", h=H), ACT.Copy)
                a.activation(qs[:, par, H, :], kv_ps[:, 0:DH], ACT.Copy)
                a.activation(v_raw[:, at(t), :], kv_ps[:, DH:2 * DH].unsqueeze(1), ACT.Copy).then_inc(q_taken, 1)

            def squares(t):
                wait(a, q_taken, of(t, 1, 1))
                wait(a, ss_ready, of(t, 1))
                a.activation(sq[:, :, :], qs[:, t[1] % 2, :, :], ACT.Square).then_inc(sq_ready, 1)

            def roots(t):
                wait(a, ss_ready, of(t, 1, 1))
                wait(a, qn_ready, of(t, 1))
                a.activation(nrm[:, :], ss[:, :], ACT.Sqrt).then_inc(nrm_ready, 1)

            def high_halves(t):
                par = t[1] % 2
                wait(a, qn_ready if cosine else q_taken, of(t, 1, 1))
                wait(a, turned[0], of(t, per[0], -per[0]))
                wait(a, turned[1], of(t, per[1], -per[1]))
                a.activation(QR[:, par, 0:H, 0:DH], qn[:, par, 0:H, :], ACT.Copy).then_inc(q_hi, 1)
                wait(a, kn_ready, of(t, 1, 1))
                a.activation(QR[:, par, H, 0:DH], kn[:, par, :], ACT.Copy)
                a.activation(QR[:, par, H, DH:P], kn[:, par, :], ACT.Copy).then_inc(k_hi, 1)

            def empty(t):
                par = t[1] % 2
                for j, g in enumerate((0, 2)):
                    wait(a, turned[0], of(t, per[0], j + 1))
                    if j == 0:
                        wait(a, q_stored[par], t[0] * 16 + t[1] // 2 * 16)
                    a.activation(qTs[:, par, 4 * g:4 * g + 4, :], tr_ps[:, 0, :].rearrange("p (a n) -> p a n", a=4),
                                 ACT.Copy).then_inc(emptied[0], 1)
                wait(a, turned[0], of(t, per[0], 3))
                a.activation(K1[:, at(t, P)], tr_ps[:, 0, 0:P], ACT.Copy)
                a.activation(K2[:, at(t, P)], tr_ps[0:DH + 1, 0, P:2 * P], ACT.Copy).then_inc(emptied[0], 1)

            if cosine:
                pipelined(a, NT, [(take_x, 3), (high_halves, 0), (squares, 1), (empty, 0), (roots, 1), (take_qkv, 2)])
            else:
                pipelined(a, NT, [(take_x, 3), (high_halves, 0), (empty, 0), (take_qkv, 2)])

        @block.tensor
        def _(pe):
            pe.wait_ge(w_ready, 1)

            def turn_x(t):
                par = t[1] % 2
                wait(pe, xn_ready, of(t, 1, 1))
                wait(pe, xT_ready, of(t, 1))
                for k in range(KD):
                    last = pe.transpose(x_ps[:, k * P:(k + 1) * P], xn[:, par, k * P:(k + 1) * P], ident[:, :])
                last.then_inc(x_turned, 1)

            def products(t):
                par = t[1] % 2
                wait(pe, xT_ready, of(t, 1, 1))
                wait(pe, q_taken, of(t, 1))
                for c in range(H * DH // ONE_BANK):
                    cols = slice(c * ONE_BANK, (c + 1) * ONE_BANK)
                    for k in range(KD):
                        pe.matmul(q_ps[:, cols], xT[:, par, k, :], W[:, k, cols], start=k == 0, stop=k == KD - 1)
                for k in range(KD):
                    last = pe.matmul(kv_ps[:, 0:2 * DH], xT[:, par, k, :], Wk[:, k, :], start=k == 0, stop=k == KD - 1)
                last.then_inc(q_product, 1)

            def turn_qk(t):
                par = t[1] % 2
                wait(pe, q_lo, of(t, 1, 1))
                for g in range(5):
                    bank, j = g % 2, g // 2
                    wait(pe, emptied[bank], of(t, per[bank], j))
                    for n in range(4 * g, min(4 * g + 4, H + 1)):
                        last = pe.transpose(tr_ps[:, bank, (n - 4 * g) * P:(n - 4 * g + 1) * P],
                                            QRf[:, par, n, :], ident[:, :])
                    if g == 4:
                        last = pe.transpose(tr_ps[0:DH + 1, bank, P:2 * P], QRf[:, par, H + 1, 0:DH + 1], ident[:, :])
                    last.then_inc(turned[bank], 1)

            pipelined(pe, NT, [(turn_x, 3), (products, 2), (turn_qk, 0)])
            pe.wait_ge(v_max, 2)
            pe.transpose(x_ps[0:1, 0:P], vmx[:, 3:4], ident[:, :]).then_inc(v_turned, 1)
            pe.wait_ge(v_top, 1)
            pe.matmul(x_ps[:, P:P + 1], ones[:, :], vtop[:, 1:2], start=True, stop=True).then_inc(v_spread, 1)
    sc.close()


def attend(nc, keep, tag, cosine, bias, qT_dram, o_dram):
    sc = Scope(nc, tag)
    sb, ps, sem = sc.sb, sc.ps, sc.sem
    ident, K1, K2, V, NS, NV = (keep[n] for n in ("ident", "K1", "K2", "V", "NS", "NV"))
    RING = 6
    q1 = [sb(f"q1_{b}", [P, S], F32R) for b in range(B)]
    q2 = [sb(f"q2_{b}", [DH + 1, S], F32R) for b in range(B)]
    width = S if cosine else TRI * P
    bias_sb = [sb(f"bias_{n}", [P, width]) for n in range(2)]
    prob = [sb(f"prob_{n}", [P, TRI * P]) for n in range(2)]
    pT_hi = [sb(f"pT_hi{n}", [P, ONE_BANK], F16) for n in range(RING)]
    pT_lo = [sb(f"pT_lo{n}", [P, ONE_BANK], F16) for n in range(RING)]
    nsu = [sb(f"nsu{n}", [P, RT]) for n in range(2)]
    ext = [sb(f"ext{n}", [P, RT]) for n in range(2)]
    shift = ext if cosine else [sb(f"shift{n}", [P, RT]) for n in range(2)]
    rsum = [sb(f"rsum{n}", [P, RT]) for n in range(2)]
    nexp = [sb(f"nexp{n}", [P, RT]) for n in range(2)]
    nprob = [sb(f"nprob{n}", [P, RT]) for n in range(2)]
    den = [sb(f"den{n}", [P, RT]) for n in range(2)]
    rden = [sb(f"rden{n}", [P, RT]) for n in range(2)]
    rback = [sb(f"rback{n}", [P, RT]) for n in range(2)]
    back_ready = sem("back_ready")
    nw = [sb(f"nw{n}", [P, RT]) for n in range(2)]
    o_half = sb("o_half", [P, RT, DH])
    o_null = sb("o_null", [P, RT, DH])
    o_sb = [sb(f"o_sb{n}", [P, RT, DH]) for n in range(2)]
    s_ps = [ps(f"s_ps{n}", [P, S]) for n in range(2)]
    t_ps = [ps(f"t_ps{n}", [P, ONE_BANK]) for n in range(2)]
    o_ps = ps("o_ps", [P, RT, P])
    q_in = [sem(f"q_in{b}") for b in range(B)]
    bias_in = [sem(f"bias_in{n}") for n in range(2)]
    (scored, extreme, row_added, exp_done, turned, hi_ready, lo_ready, pv_done, null_in, null_diff, null_exp,
     den_ready, rden_ready, half_taken, o_taken, o_scaled, null_weight, null_value, o_ready, ones_ready) = (
        sem(n) for n in ("scored", "extreme", "row_added", "exp_done", "turned", "hi_ready", "lo_ready", "pv_done",
                         "null_in", "null_diff", "null_exp", "den_ready", "rden_ready", "half_taken", "o_taken",
                         "o_scaled", "null_weight", "null_value", "o_ready", "ones_ready"))
    o_stored = [sem("o_stored0"), sem("o_stored1")]
    bias_masked = [sem(f"bias_masked{n}") for n in range(2)]
    order = [x for r in range(RT // 2) for x in (r, RT - 1 - r)]
    start = [sum(r + 1 for r in order[:p]) for p in range(RT + 1)]
    tiles = [(r, c) for r in order for c in range(r + 1)]
    done_after = [start[p + 1] // 4 for p in range(RT)]
    first_of = [0] + done_after[:-1]
    LAG = 2

    def g_slot(off, g):
        assert 4 * GROUPS % RING == 0
        return (GROUPS * off + g) % RING
    BIAS_DMAS = 1 if cosine else RT

    def count(u, n, c=0):
        i, off = u
        return i * (4 * n) + (off * n + c)

    def ahead(u, p, by):
        i, off = u
        return (i, off + (p + by) // RT), (p + by) % RT

    def in_steps(eng, step):
        def body(i, last):
            for off in range(4):
                for p in range(RT):
                    step((i, off), p, (RT * (4 - off) - p) if last else 99)
        in_pairs(eng, H // 2, body)

    with nc.Block() as block:
        @block.sync
        def _(sp):
            def load_bias(u):
                i, off = u
                head = i * 2 + off // 2
                buf = (off // 2) % 2
                wait_alone(sp, row_added, count(u, RT, -2 * RT))
                hs = bass.ds(head, 1) if not isinstance(head, int) else slice(head, head + 1)
                if cosine:
                    src = bias[hs, 0:P, P - 1:P - 1 + S].rearrange("a p n -> p (a n)")
                    sp.dma_start(bias_sb[buf][:, :], src).then_inc(bias_in[buf], 16)
                else:
                    for r in range(RT):
                        src = bias[hs, r * P:(r + 1) * P, 0:(r + 1) * P].rearrange("a p n -> p (a n)")
                        at = r * (r + 1) // 2 * P
                        sp.dma_start(bias_sb[buf][:, at:at + (r + 1) * P], src).then_inc(bias_in[buf], 16)

            def load_q(u):
                i, off = u
                head = i * 2 + off // 2
                b = off % 2
                wait_alone(sp, scored, count(u, RT, -RT))
                hs = bass.ds(head, 1) if not isinstance(head, int) else slice(head, head + 1)
                src = qT_dram[hs, :, b * S:(b + 1) * S]
                sp.dma_start(q1[b][:, :].bitcast(F32), src.rearrange("a p n -> p (a n)")).then_inc(q_in[b], 16)
                sp.dma_start(q2[b][0:DH, :].bitcast(F32), src[:, 0:DH, :].rearrange("a p n -> p (a n)")).then_inc(q_in[b], 16)

            def body(i, last):
                for off in range(4):
                    u = (i, off)
                    if off % 2 == 0 and not (last and off == 2):
                        load_bias((i, off + 2))
                    if not (last and off >= 2):
                        load_q((i, off + 2))
                    wait_alone(sp, o_ready, count(u, 1, 1))
                    head, b = i * 2 + off // 2, off % 2
                    cols = bass.ds(head * DH, DH) if not isinstance(head, int) else slice(head * DH, (head + 1) * DH)
                    sp.dma_start(o_dram[b * RT:(b + 1) * RT, :, cols].rearrange("t p n -> p t n"),
                                 o_sb[b][:, :, :]).then_inc(o_stored[b], 16)
            load_bias((0, 0))
            load_q((0, 0))
            load_q((0, 1))
            in_pairs(sp, H // 2, body)
            for b in range(B):
                sp.wait_ge(o_stored[b], 16 * H)

        @block.tensor
        def _(pe):
            pe.wait_ge(ones_ready, 1)

            def scores(u, p):
                off = u[1]
                b, r = off % 2, order[p]
                if p == 0:
                    wait(pe, q_in[b], u[0] * 64 + (off // 2 + 1) * 32)
                wait(pe, row_added, count(u, RT, p - 1))
                n = (r + 1) * P
                for c in range(0, n, ONE_BANK):
                    w = min(ONE_BANK, n - c)
                    pe.matmul(s_ps[p % 2][:, c:c + w], q1[b][:, r * P:(r + 1) * P],
                              K1[:, b * S + c:b * S + c + w], start=True, stop=False)
                    last = pe.matmul(s_ps[p % 2][:, c:c + w], q2[b][:, r * P:(r + 1) * P],
                                     K2[:, b * S + c:b * S + c + w], start=False, stop=True)
                last.then_inc(scored, 1)

            def turn(u, p):
                i, off = u
                wait(pe, exp_done, count(u, RT, p + 1))
                for s in range(start[p], start[p + 1]):
                    g, j = divmod(s, 4)
                    bank = (GROUPS * off + g) % 2
                    if j == 0:
                        wait(pe, lo_ready, count(u, GROUPS, g - 1))
                    last = pe.transpose(t_ps[bank][:, j * P:(j + 1) * P], prob[off % 2][:, s * P:(s + 1) * P], ident[:, :])
                    if j == 3:
                        last.then_inc(turned, 1)
                        if g >= LAG:
                            weigh(u, g - LAG)
                        elif not very_first(u):
                            weigh((i, off - 1), GROUPS + g - LAG)

            def weigh(u, g):
                off = u[1]
                b = off % 2
                slot = g_slot(off, g)
                if g == 0:
                    wait(pe, o_taken, count(u, 1))
                wait(pe, lo_ready, count(u, GROUPS, g + 1))
                for j in range(4):
                    r, c = tiles[4 * g + j]
                    pe.matmul(o_ps[:, r, :], pT_hi[slot][:, j * P:(j + 1) * P], V[:, b * RT + c, :],
                              start=c == 0, stop=False)
                    last = pe.matmul(o_ps[:, r, :], pT_lo[slot][:, j * P:(j + 1) * P], V[:, b * RT + c, :],
                                     start=False, stop=c == r)
                last.then_inc(pv_done, 1)

            def step(u, p, left):
                if left > 2:
                    scores(*ahead(u, p, 2))
                turn(u, p)
            scores((0, 0), 0)
            scores((0, 0), 1)
            in_steps(pe, step)
            for g in range(GROUPS - LAG, GROUPS):
                weigh((H // 2 - 1, 3), g)

        @block.vector
        def _(v):
            for b in range(B):
                last = v.memset(q2[b][DH:DH + 1, :].bitcast(F32), 1.0)
            last.then_inc(ones_ready, 1)

            def add(u, p):
                off = u[1]
                par, buf, r = off % 2, (off // 2) % 2, order[p]
                n = (r + 1) * P
                at = start[p] * P
                if p == 0:
                    wait(v, null_in, count(u, 1, 1))
                    if off % 2 == 0:
                        turn_of = u[0] + (off // 4 + 1)
                        if cosine:
                            wait(v, bias_in[buf], turn_of * 16)
                        else:
                            wait(v, bias_masked[buf], turn_of * RT)
                    wait(v, turned, count(u, GROUPS, -GROUPS))
                    wait(v, null_diff, count(u, 1, -1))
                wait_alone(v, scored, count(u, RT, p + 1))
                tri = r * (r + 1) // 2 * P
                src = bias_sb[buf][:, (RT - 1 - r) * P:S] if cosine else bias_sb[buf][:, tri:tri + n]
                ins = v.tensor_tensor_reduce(out=prob[par][:, at:at + n], in0=s_ps[p % 2][:, 0:n], in1=src,
                                             scale=1.0, scalar=nsu[par][:, r:r + 1], op0=ALU.add,
                                             op1=ALU.min if cosine else ALU.max, accum_out=ext[par][:, r:r + 1])
                if cosine:
                    ins.then_inc(row_added, 1)
                else:
                    ins.then_inc(extreme, 1)
                    wait(v, extreme, count(u, RT, p + 1))
                    v.tensor_scalar(shift[par][:, r:r + 1], ext[par][:, r:r + 1], -1.0, None,
                                    ALU.mult).then_inc(row_added, 1)

            def split(u, g):
                off = u[1]
                slot, bank = g_slot(off, g), (GROUPS * off + g) % 2
                wait(v, hi_ready, count(u, GROUPS, g + 1))
                wait(v, pv_done, count(u, GROUPS, g + 1 - RING))
                v.scalar_tensor_tensor(out=pT_lo[slot][:, :], in0=t_ps[bank][:, :], scalar=P_SCALE,
                                       in1=pT_hi[slot][:, :], op0=ALU.mult, op1=ALU.subtract).then_inc(lo_ready, 1)

            def finish(u):
                par = u[1] % 2
                wait(v, den_ready, count(u, 1, 1))
                v.reciprocal(rden[par][:, :], den[par][:, :]).then_inc(rden_ready, 1)
                wait(v, half_taken, count(u, 1, 1))
                wait(v, o_stored[par], u[0] * 32 + (u[1] // 2) * 16)
                v.tensor_tensor(o_sb[par][:, :, :], o_ps[:, :, 0:DH], o_half[:, :, :], ALU.add).then_inc(o_taken, 1)

            def step(u, p, left):
                if left > 2:
                    add(*ahead(u, p, 2))
                for g in range(first_of[p], done_after[p]):
                    split(u, g)
                if p == 1 and not very_first(u):
                    finish((u[0], u[1] - 1))
            add((0, 0), 0)
            add((0, 0), 1)
            in_steps(v, step)
            finish((H // 2 - 1, 3))

        @block.scalar
        def _(a):
            def exps(u, p):
                par, r = u[1] % 2, order[p]
                at = start[p] * P
                n = (r + 1) * P
                if p == 0:
                    wait(a, den_ready, count(u, 1, -1))
                wait(a, row_added, count(u, RT, p + 1))
                a.activation(prob[par][:, at:at + n], prob[par][:, at:at + n], ACT.Exp,
                             bias=shift[par][:, r:r + 1], scale=-1.0 if cosine else 1.0,
                             accum_out=rsum[par][:, r:r + 1]).then_inc(exp_done, 1)

            def split(u, g):
                off = u[1]
                slot, bank = g_slot(off, g), (GROUPS * off + g) % 2
                wait(a, turned, count(u, GROUPS, g + 1))
                wait(a, pv_done, count(u, GROUPS, g + 1 - RING))
                a.activation(pT_hi[slot][:, :], t_ps[bank][:, :], ACT.Copy, scale=P_SCALE).then_inc(hi_ready, 1)

            def finish(u):
                par = u[1] % 2
                wait(a, null_diff, count(u, 1, 1))
                wait(a, null_weight, count(u, 1, -1))
                a.activation(nexp[par][:, :], nprob[par][:, :], ACT.Exp).then_inc(null_exp, 1)
                wait(a, pv_done, count(u, GROUPS, GROUPS))
                wait(a, o_taken, count(u, 1))
                a.activation(o_half[:, :, :], o_ps[:, :, DH:2 * DH], ACT.Copy).then_inc(half_taken, 1)

            def step(u, p, left):
                if left > 1:
                    exps(*ahead(u, p, 1))
                for g in range(first_of[p], done_after[p]):
                    split(u, g)
                if p == 1 and not very_first(u):
                    finish((u[0], u[1] - 1))
            exps((0, 0), 0)
            in_steps(a, step)
            finish((H // 2 - 1, 3))

        @block.gpsimd
        def _(pool):
            def null_scores(u):
                i, off = u
                head, b = i * 2 + off // 2, off % 2
                wait(pool, row_added, count(u, RT, -RT))
                hs = bass.ds(head, 1) if not isinstance(head, int) else slice(head, head + 1)
                src = NS[:, hs, b * RT:(b + 1) * RT].rearrange("p a n -> p (a n)")
                pool.tensor_copy(nsu[off % 2][:, :], src).then_inc(null_in, 1)

            def mask_bias(u):
                i, off = u
                buf = (off // 2) % 2
                wait_alone(pool, bias_in[buf], i * (16 * RT) + (off // 4 + 1) * 16 * RT)
                for r in range(RT):
                    at = (r * (r + 1) // 2 + r) * P
                    tile = bias_sb[buf][:, at:at + P]
                    pool.affine_select(out=tile, in_=tile, compare_op=ALU.is_ge, fill=-BIG, base=0,
                                       pattern=[[-1, P]], channel_multiplier=1).then_inc(bias_masked[buf], 1)

            def body(i, last):
                for off in range(4):
                    u = (i, off)
                    par = off % 2
                    if not cosine and off % 2 and not (last and off == 3):
                        mask_bias((i, off + 1))
                    wait(pool, row_added, count(u, RT, RT))
                    wait(pool, null_exp, count(u, 1, -1))
                    if cosine:
                        pool.tensor_tensor(nprob[par][:, :], ext[par][:, :], nsu[par][:, :], ALU.subtract).then_inc(null_diff, 1)
                    else:
                        pool.tensor_tensor(nprob[par][:, :], shift[par][:, :], nsu[par][:, :], ALU.add).then_inc(null_diff, 1)
                    if not (last and off >= 2):
                        wait(pool, null_diff, count(u, 1, 1))
                        null_scores((i, off + 2))
                    wait(pool, null_exp, count(u, 1, 1))
                    wait(pool, exp_done, count(u, RT, RT))
                    wait(pool, rden_ready, count(u, 1, -1))
                    pool.tensor_tensor(den[par][:, :], rsum[par][:, :], nexp[par][:, :], ALU.add).then_inc(den_ready, 1)
                    wait(pool, rden_ready, count(u, 1, 1))
                    pool.tensor_tensor(nw[par][:, :], nexp[par][:, :], rden[par][:, :], ALU.mult).then_inc(null_weight, 1)
                    pool.tensor_tensor(rback[par][:, :], rden[par][:, :], keep["v_back"][:, :].to_broadcast([P, RT]),
                                       ALU.mult).then_inc(back_ready, 1)
                    wait(pool, null_weight, count(u, 1, 1))
                    wait(pool, o_ready, count(u, 1))
                    pool.tensor_tensor(o_null[:, :, :], spread(nw[par][:, :], DH), repeat(NV[:, :], RT), ALU.mult).then_inc(null_value, 1)
                    wait(pool, o_taken, count(u, 1, 1))
                    wait(pool, back_ready, count(u, 1, 1))
                    pool.tensor_tensor(o_sb[par][:, :, :], o_sb[par][:, :, :], spread(rback[par][:, :], DH), ALU.mult).then_inc(o_scaled, 1)
                    wait(pool, null_value, count(u, 1, 1))
                    wait(pool, o_scaled, count(u, 1, 1))
                    pool.tensor_tensor(o_sb[par][:, :, :], o_sb[par][:, :, :], o_null[:, :, :], ALU.add).then_inc(o_ready, 1)
            if not cosine:
                mask_bias((0, 0))
            null_scores((0, 0))
            null_scores((0, 1))
            in_pairs(pool, H // 2, body)
    sc.close()


def merge(nc, keep, tag, Wout, g_out, o_dram):
    sc = Scope(nc, tag)
    sb, ps, sem = sc.sb, sc.ps, sc.sem
    ident, X = keep["ident"], keep["X"]
    JT = H * DH // P
    W = sb("W", [P, JT, D])
    gr = sb("gr", [P, D])
    eps = sb("eps", [P, 1])
    o = sb("o", [P, 2, H * DH])
    oT = sb("oT", [P, 2, JT, P])
    stat = sb("stat", [P, 6])
    mv = sb("mv", [P, 2, 2])
    std = sb("std", [P, 2])
    rstd = sb("rstd", [P, 1])
    y = sb("y", [P, D])
    yg = sb("yg", [P, D])
    t_ps = ps("t_ps", [P, 2, H * DH])
    y_ps = ps("y_ps", [P, 2, ONE_BANK])
    params, o_in, turned, oT_a, oT_v, product, stats, var_ready, std_ready, chain, added, eps_ready = (
        sem(n) for n in ("params", "o_in", "turned", "oT_a", "oT_v", "product", "stats", "var_ready",
                         "std_ready", "chain", "added", "eps_ready"))
    o_in = [sem("o_in0"), sem("o_in1")]
    LINKS = 3

    with nc.Block() as block:
        @block.sync
        def _(sp):
            sp.dma_start(W[:, :, :], Wout.rearrange("(j p) n -> p j n", p=P)).then_inc(params, 16)
            sp.dma_start(gr[:, :], row_of(g_out, D)).then_inc(params, 16)

            def load(t):
                par = t[1] % 2
                wait_alone(sp, turned, of(t, 1, -1))
                sp.dma_start(o[:, par, :], o_dram[at(t), :, :].rearrange("a p n -> p (a n)")).then_inc(o_in[par], 16)
            pipelined(sp, NT, [(load, 0)])

        @block.tensor
        def _(pe):
            pe.wait_ge(params, 32)

            def turn(t):
                par = t[1] % 2
                wait(pe, o_in[par], t[0] * 16 + (t[1] // 2 + 1) * 16)
                wait(pe, oT_a, of(t, 1, -1))
                wait(pe, oT_v, of(t, 1, -1))
                for j in range(JT):
                    last = pe.transpose(t_ps[:, par, j * P:(j + 1) * P], o[:, par, j * P:(j + 1) * P], ident[:, :])
                last.then_inc(turned, 1)

            def products(t):
                par = t[1] % 2
                wait(pe, oT_a, of(t, 1, 1))
                wait(pe, oT_v, of(t, 1, 1))
                wait(pe, chain, of(t, LINKS, -2 * LINKS + 2))
                for j in range(JT):
                    last = pe.matmul(y_ps[:, par, 0:D], oT[:, par, j, :], W[:, j, :], start=j == 0, stop=j == JT - 1)
                last.then_inc(product, 1)
            pipelined(pe, NT, [(turn, 1), (products, 0)])

        @block.scalar
        def _(a):
            a.wait_ge(eps_ready, 1)

            def take(t):
                off = t[1] % 2
                wait(a, turned, of(t, 1, 1))
                wait(a, product, of(t, 1, -1))
                a.activation(oT[:, off, 0:JT // 2, :], t_ps[:, off, 0:JT // 2 * P].rearrange("p (j n) -> p j n", n=P),
                             ACT.Copy).then_inc(oT_a, 1)

            def root(t):
                off = t[1] % 2
                wait(a, var_ready, of(t, 1, 1))
                a.activation(std[:, off:off + 1], mv[:, off, 1:2], ACT.Sqrt, bias=eps[:, :]).then_inc(std_ready, 1)

            pipelined(a, NT, [(take, 1), (root, -1)])

        @block.vector
        def _(v):
            v.memset(eps[:, :], EPS).then_inc(eps_ready, 1)

            def take(t):
                off = t[1] % 2
                wait(v, turned, of(t, 1, 1))
                wait(v, product, of(t, 1, -1))
                v.tensor_copy(oT[:, off, JT // 2:JT, :],
                              t_ps[:, off, JT // 2 * P:JT * P].rearrange("p (j n) -> p j n", n=P)).then_inc(oT_v, 1)

            def norm(t):
                off = t[1] % 2
                wait(v, product, of(t, 1, 1))
                v.bn_stats(stat[:, :], y_ps[:, off, 0:D]).then_inc(stats, 1)
                wait_alone(v, stats, of(t, 1, 1))
                v.bn_aggr(mv[:, off, :], stat[:, :]).then_inc(var_ready, 1)
                wait(v, std_ready, of(t, 1, 1))
                v.reciprocal(rstd[:, :], std[:, off:off + 1]).then_inc(chain, 1)
                wait(v, chain, of(t, LINKS, 1))
                v.tensor_scalar(y[:, :], y_ps[:, off, 0:D], mv[:, off, 0:1], rstd[:, :], ALU.subtract, ALU.mult).then_inc(chain, 1)
                wait(v, chain, of(t, LINKS, 2))
                v.tensor_tensor(yg[:, :], y[:, :], gr[:, :], ALU.mult).then_inc(chain, 1)
                wait(v, chain, of(t, LINKS, 3))
                Xt = X[:, at(t), :].rearrange("p a n -> p (a n)")
                v.tensor_tensor(Xt, Xt, yg[:, :], ALU.add).then_inc(added, 1)

            pipelined(v, NT, [(take, 1), (norm, -1)])
    sc.close()


def experts(nc, keep, tag, cond, wt, wg, w_gate, w_up, w_down, sw_gate, sw_up, sw_down):
    sc = Scope(nc, tag)
    sb, ps, sem = sc.sb, sc.ps, sc.sem
    ident, X = keep["ident"], keep["X"]
    SM = 2 * M
    MT = E + SM // M
    CT = 4
    CH = NT // CT
    CW = CT * P
    GD = 64
    wgate = sb("wgate", [P, KD, MT, M])
    wup = sb("wup", [P, KD, MT, M])
    wdown = sb("wdown", [P, MT, D])
    wtT_in = sb("wtT_in", [E, D])
    wgT_in = sb("wgT_in", [E, GD])
    g_in = sb("g_in", [B, GD])
    wtT = sb("wtT", [P, KD, E])
    wgT = sb("wgT", [GD, E])
    gT = sb("gT", [GD, B, P])
    route = sb("route", [P, NT, E])
    top = sb("top", [P, NT, E])
    idx = sb("idx", [P, NT, E], U32)
    idxf = sb("idxf", [P, NT, E])
    lanes_i = sb("lanes_i", [P, E], I32)
    lanes = sb("lanes", [P, E])
    work = sb("work", [P, NT, E])
    z = sb("z", [P, NT])
    s12 = sb("s12", [P, NT, 2])
    sden = sb("sden", [P, NT])
    pick = sb("pick", [P, 2, NT, E])
    xT = sb("xT", [P, KD, NT * P])
    gate_sb = sb("gate_sb", [P, 2, CW])
    act_sb = sb("act_sb", [P, 2, CW])
    hid = sb("hid", [P, MT, CW])
    acc = sb("acc", [P, 2, D])
    pg = ps("pg", [P, 2, CW])
    pu = ps("pu", [P, 2, CW])
    py = ps("py", [P, 4, ONE_BANK])
    NW = 9
    params, turned, taken, lanes_made, logit, dve0, expd, routed = (
        sem(n) for n in ("params", "turned", "taken", "lanes_made", "logit", "dve0", "expd", "routed"))
    hidden, gate_taken, leaky, up_used, down, summed, x_taken, pair_taken = (
        sem(n) for n in ("hidden", "gate_taken", "leaky", "up_used", "down", "summed", "x_taken", "pair_taken"))
    marks = {}

    with nc.Block() as block:
        @block.sync
        def _(sp):
            sp.dma_start(wtT_in[:, :], wt).then_inc(params, 16)
            sp.dma_start(wgT_in[:, :], wg).then_inc(params, 16)
            sp.dma_start(g_in[:, :], cond).then_inc(params, 16)
            for k in range(KD):
                rows = slice(k * P, (k + 1) * P)
                for dst, many, shared in ((wgate, w_gate, sw_gate), (wup, w_up, sw_up)):
                    sp.dma_start(dst[:, k, 0:E, :], many[:, rows, :].rearrange("e p m -> p e m")).then_inc(params, 16)
                    sp.dma_start(dst[:, k, E:MT, :], shared[rows, :].rearrange("p (e m) -> p e m", m=M)).then_inc(params, 16)
            sp.dma_start(wdown[:, 0:E, :], w_down.rearrange("e p n -> p e n")).then_inc(params, 16)
            sp.dma_start(wdown[:, E:MT, :], sw_down.rearrange("(e p) n -> p e n", p=P)).then_inc(params, 16)

        ALL = 16 * (3 + 4 * KD + 2)

        @block.gpsimd
        def _(pool):
            pool.iota(lanes_i[:, :], [[1, E]], base=0, channel_multiplier=0).then_inc(lanes_made, 1)

        @block.tensor
        def _(pe):
            pe.wait_ge(params, ALL)
            for k in range(KD):
                pe.transpose(py[:, 0, k * E:(k + 1) * E], wtT_in[:, k * P:(k + 1) * P], ident[0:E, 0:E])
            pe.transpose(py[0:GD, 0, 64:64 + E], wgT_in[:, :], ident[0:E, 0:E])
            pe.transpose(py[0:GD, 0, 128:128 + B], g_in[:, :], ident[0:B, 0:B]).then_inc(turned, 1)
            for t in range(NT):
                wait(pe, taken, t - 1 + 1 if t >= 2 else 0)
                for k in range(KD):
                    last = pe.transpose(pg[:, t % 2, k * P:(k + 1) * P], X[:, t, k * P:(k + 1) * P], ident[:, :])
                last.then_inc(turned, 1)
            pe.wait_ge(taken, NT + 1)
            pe.wait_ge(x_taken, 1)
            for t in range(NT):
                for k in range(KD):
                    pe.matmul(py[:, 1, t * E:(t + 1) * E], xT[:, k, t * P:(t + 1) * P], wtT[:, k, :], start=k == 0, stop=False)
                last = pe.matmul(py[:, 1, t * E:(t + 1) * E], gT[:, t // RT, :], wgT[:, :], start=False, stop=True)
            last.then_inc(logit, 1)

            def chunk(i):
                for m in range(MT):
                    bank = m % 2
                    wait(pe, gate_taken, i * MT + m - 1)
                    wait(pe, up_used, i * MT + m - 1)
                    for out, w in ((pg, wgate), (pu, wup)):
                        for k in range(KD):
                            cols = slice(i * CW, (i + 1) * CW) if isinstance(i, int) else bass.ds(i * CW, CW)
                            last = pe.matmul(out[:, bank, :], w[:, k, m, :], xT[:, k, cols], start=k == 0, stop=k == KD - 1)
                    last.then_inc(hidden, 1)
                wait(pe, up_used, i * MT + MT)
                for c in range(CT):
                    for m in range(E + 1):
                        n = c * (E + 1) + m
                        wait(pe, summed, i * (CT * (E + 1)) + n - 3)
                        if isinstance(i, int) and n == 1:
                            pe.wait_ge(routed, 1)
                        parts = [m] if m < E else range(E, MT)
                        for q in parts:
                            last = pe.matmul(py[:, n % 4, 0:D], hid[:, q, c * P:(c + 1) * P], wdown[:, q, :],
                                             start=q == parts[0], stop=q == parts[-1])
                        last.then_inc(down, 1)
            chunk(0)
            with pe.Fori(1, CH) as i:
                chunk(i)

        @block.scalar
        def _(a):
            for t in range(NT):
                a.wait_ge(turned, t + 2)
                a.activation(xT[:, :, t * P:(t + 1) * P], pg[:, t % 2, 0:KD * P].rearrange("p (k n) -> p k n", k=KD),
                             ACT.Copy).then_inc(taken, 1)
            a.sem_inc(taken, 1)
            a.wait_ge(dve0, marks_at("shifted"))
            a.activation(work[:, :, :], work[:, :, :], ACT.Exp).then_inc(expd, 1)

            def chunk(i):
                for m in range(MT):
                    wait(a, hidden, i * MT + m + 1)
                    wait(a, leaky, i * MT + m - 1)
                    a.activation(gate_sb[:, m % 2, :], pg[:, m % 2, :], ACT.Copy).then_inc(gate_taken, 1)
            chunk(0)
            with a.Fori(1, CH) as i:
                chunk(i)

        @block.vector
        def _(v):
            done = [0]

            def link(ins, name=None):
                done[0] += 1
                ins.then_inc(dve0, 1)
                v.wait_ge(dve0, done[0])
                if name:
                    assert marks_at(name) == done[0], done[0]

            v.wait_ge(lanes_made, 1)
            link(v.tensor_copy(lanes[:, :], lanes_i[:, :]))
            v.wait_ge(turned, 1)
            for k in range(KD):
                v.tensor_copy(wtT[:, k, :], py[:, 0, k * E:(k + 1) * E])
            v.tensor_copy(wgT[:, :], py[0:GD, 0, 64:64 + E])
            last = None
            for b in range(B):
                last = v.tensor_copy(gT[:, b, :], py[0:GD, 0, 128 + b:129 + b].to_broadcast([GD, P]))
            last.then_inc(x_taken, 1)
            v.wait_ge(logit, 1)
            link(v.tensor_scalar(route[:, :, :], py[:, 1, 0:NT * E].rearrange("p (t e) -> p t e", e=E), 0.5, None, ALU.mult))
            for t in range(NT):
                last = v.max(top[:, t, :], route[:, t, :])
            link(last)
            for t in range(NT):
                last = v.max_index(idx[:, t, :], top[:, t, :], route[:, t, :])
            link(last)
            link(v.tensor_copy(idxf[:, :, :], idx[:, :, :]))
            link(v.tensor_tensor(work[:, :, :], top[:, :, :], spread(top[:, :, 0], E), ALU.subtract), "shifted")
            v.wait_ge(expd, 1)
            link(v.tensor_reduce(z[:, :], work[:, :, :], AX_X, ALU.add))
            link(v.reciprocal(z[:, :], z[:, :]))
            link(v.tensor_tensor(s12[:, :, :], work[:, :, 0:2], spread(z[:, :], 2), ALU.mult))
            link(v.tensor_tensor(sden[:, :], s12[:, :, 0], s12[:, :, 1], ALU.add))
            link(v.tensor_scalar(sden[:, :], sden[:, :], 1e-20, None, ALU.add))
            link(v.reciprocal(sden[:, :], sden[:, :]))
            link(v.tensor_tensor(s12[:, :, :], s12[:, :, :], spread(sden[:, :], 2), ALU.mult))
            for n in range(2):
                link(v.tensor_tensor(pick[:, n, :, :], repeat(lanes[:, :], NT), spread(idxf[:, :, n], E), ALU.is_equal))
                link(v.tensor_tensor(pick[:, n, :, :], pick[:, n, :, :], spread(s12[:, :, n], E), ALU.mult))
            link(v.tensor_tensor(work[:, :, :], pick[:, 0, :, :], pick[:, 1, :, :], ALU.add))
            v.tensor_copy(route[:, :, :], work[:, :, :]).then_inc(routed, 1)

            def chunk(i):
                for m in range(MT):
                    n = i * MT + m
                    wait(v, gate_taken, n + 1)
                    v.scalar_tensor_tensor(out=act_sb[:, m % 2, :], in0=gate_sb[:, m % 2, :], scalar=0.01,
                                           in1=gate_sb[:, m % 2, :], op0=ALU.mult, op1=ALU.max).then_inc(leaky, 1)
                    wait(v, leaky, n + 1)
                    if m == 0:
                        wait(v, down, i * (CT * (E + 1)))
                    v.tensor_tensor(hid[:, m, :], act_sb[:, m % 2, :], pu[:, m % 2, :], ALU.mult).then_inc(up_used, 1)
                if isinstance(i, int) and i == 0:
                    v.wait_ge(routed, 1)
                for c in range(CT):
                    at = slice(i * CT + c, i * CT + c + 1) if isinstance(i, int) else bass.ds(i * CT + c, 1)
                    Xt = X[:, at, :].rearrange("p a n -> p (a n)")
                    for m in range(E + 1):
                        n = c * (E + 1) + m
                        wait(v, down, i * (CT * (E + 1)) + n + 1)
                        wait(v, summed, i * (CT * (E + 1)) + n)
                        if m < E:
                            v.scalar_tensor_tensor(out=Xt, in0=py[:, n % 4, 0:D],
                                                   scalar=route[:, at, m:m + 1].rearrange("p a n -> p (a n)"),
                                                   in1=Xt, op0=ALU.mult, op1=ALU.add).then_inc(summed, 1)
                        else:
                            v.tensor_tensor(Xt, py[:, n % 4, 0:D], Xt, ALU.add).then_inc(summed, 1)
            chunk(0)
            with v.Fori(1, CH) as i:
                chunk(i)
    sc.close()


def marks_at(name):
    return {"shifted": 6}[name]


def program(nc, t, out):
    with ExitStack() as ctx:
        def sb(name, shape, dt=F32):
            return ctx.enter_context(nc.sbuf_tensor(name, shape, dt))
        keep = {
            "ident": sb("ident", [P, P]), "X": sb("X", [P, NT, D]),
            "K1": sb("K1", [P, B * S], F32R), "K2": sb("K2", [DH + 1, B * S], F32R),
            "V": sb("V", [P, NT, 2 * DH], F16), "v_back": sb("v_back", [P, 1]), "NS": sb("NS", [P, H, NT]), "NV": sb("NV", [P, DH]),
        }
        shifted = nc.dram_tensor("shifted", (H, P + 1, PITCH), F32, kind="Internal").ap()
        qT_dram = nc.dram_tensor("qT", (H, P, B * S), F32, kind="Internal").ap()
        o_dram = nc.dram_tensor("o", (NT, P, H * DH), F32, kind="Internal").ap()
        x_tiles = t["x"].rearrange("b (t p) d -> p (b t) d", p=P)
        out_tiles = out.rearrange("b (t p) d -> p (b t) d", p=P)

        sc = Scope(nc, "start")
        x_in, zeroed = sc.sem("x_in"), sc.sem("zeroed")
        with nc.Block() as block:
            @block.sync
            def _(sp):
                sp.dma_start(keep["X"][:, :, :], x_tiles).then_inc(x_in, 16)
                sp.wait_ge(x_in, 16)

            @block.gpsimd
            def _(pool):
                pool.memset(keep["ident"][:, :], 0.0).then_inc(zeroed, 1)
                pool.wait_ge(zeroed, 1)
                pool.affine_select(out=keep["ident"][:, :], in_=keep["ident"][:, :], compare_op=ALU.not_equal,
                                   fill=1.0, base=0, pattern=[[-1, P]], channel_multiplier=1).then_inc(zeroed, 1)
                pool.wait_ge(zeroed, 2)
        sc.close()

        def cosine_layer(L, mask):
            g = lambda n: t[f"{L}_cond_{n}"]
            bias_tables(nc, keep, f"{L}t", g("w0"), g("b0"), g("g0"), g("w1"), g("b1"), g("g1"), g("w2"), g("b2"), shifted)
            project(nc, keep, f"{L}p", True, g("Wq"), g("Wkv"), g("g_norm"), g("q_scale"), g("k_scale"),
                    g("null_attn_bias"), t["cond_64"], mask, qT_dram)
            attend(nc, keep, f"{L}a", True, shifted, qT_dram, o_dram)
            merge(nc, keep, f"{L}m", g("Wout"), g("g_out"), o_dram)

        cosine_layer("L0", t["mask_BxS_bf1"])
        g = lambda n: t[f"L1_cond_{n}"]
        experts(nc, keep, "L1", t["cond_64"], g("wt"), g("wg"), g("w_gate"), g("w_up"), g("w_down"),
                g("sw_gate"), g("sw_up"), g("sw_down"))
        g2 = lambda n: t[f"L2_cond_{n}"]
        project(nc, keep, "L2p", False, g2("Wq"), g2("Wkv"), g2("g_in"), None, None, g2("null_attn_bias"),
                t["cond_64"], t["mask_BxS_bk0"], qT_dram)
        attend(nc, keep, "L2a", False, t["fside_16xSxS_0"], qT_dram, o_dram)
        merge(nc, keep, "L2m", g2("Wo"), g2("g_out"), o_dram)
        cosine_layer("L3", t["mask_BxS_bf1"])

        sc = Scope(nc, "end")
        x_out = sc.sem("x_out")
        with nc.Block() as block:
            @block.sync
            def _(sp):
                sp.dma_start(out_tiles, keep["X"][:, :, :]).then_inc(x_out, 16)
                sp.wait_ge(x_out, 16)
        sc.close()


def kernel(**inputs):
    import concourse.bacc as bacc
    from concourse.bass_utils import run_bass_kernel_spmd

    nc = bacc.Bacc("TRN2", target_bir_lowering=False, num_devices=1)
    arrays, args = {}, {}
    for name, value in inputs.items():
        a = np.ascontiguousarray(value)
        arrays[f"in_{name}"] = a
        args[name] = nc.dram_tensor(f"in_{name}", a.shape, mybir.dt.from_np(a.dtype), kind="ExternalInput").ap()
    out = nc.dram_tensor("out", (B, S, D), F32, kind="ExternalOutput").ap()
    program(nc, args, out)
    r = run_bass_kernel_spmd(nc, [arrays], core_ids=[0])
    return r.results[0]["out"]
```

```python
from contextlib import ExitStack

import numpy as np
import concourse.bass as bass
from concourse import mybir

F32 = mybir.dt.float32
F32R = mybir.dt.float32r
F16 = mybir.dt.float16
I32 = mybir.dt.int32
U32 = mybir.dt.uint32
U8 = mybir.dt.uint8
ALU = mybir.AluOpType
ACT = mybir.ActivationFunctionType
AX_X = mybir.AxisListType.X
AX_XY = mybir.AxisListType.XY

P = 128
B, S, D = 2, 1024, 256
H, DH = 16, 64
KD = D // P
NT = B * S // P
RT = S // P
TRI = RT * (RT + 1) // 2
GROUPS = TRI // 4
E, M = 8, 128
BIG = float(2 ** 100)
EPS = 1e-5
PITCH = S + P
HEADS_AT_ONCE = 4
ONE_BANK = 512
P_SCALE = float(2 ** 15)
V_SCALE = float(2 ** 14)


def wait(eng, sem, value):
    if isinstance(value, int) and value <= 0:
        return
    eng.wait_ge(sem, value)


def wait_alone(eng, sem, value):
    if isinstance(value, int):
        if value > 0:
            eng.wait_ge(sem, value)
        return
    eng.wait_ge(sem, value)
    eng.nop(nofuse=True)


def row_of(ap, n, parts=P):
    return bass.AP(tensor=ap.tensor, offset=ap.offset, ap=[[0, parts], [1, n]])


def spread(ap, n):
    return ap.unsqueeze(2).to_broadcast([ap.shape[0], ap.shape[1], n])


def repeat(ap, n):
    return ap.unsqueeze(1).to_broadcast([ap.shape[0], n, ap.shape[1]])


def very_first(u):
    return isinstance(u[0], int) and u[0] == 0 and u[1] == 0


class Scope:

    def __init__(self, nc, tag):
        self.nc, self.tag, self.ctx, self.sems = nc, tag, ExitStack(), []

    def sb(self, name, shape, dt=F32):
        return self.ctx.enter_context(self.nc.sbuf_tensor(f"{self.tag}_{name}", shape, dt))

    def ps(self, name, shape, dt=F32):
        return self.ctx.enter_context(self.nc.psum_tensor(f"{self.tag}_{name}", shape, dt))

    def sem(self, name):
        s = self.ctx.enter_context(self.nc.semaphore(f"{self.tag}_{name}"))
        self.sems.append(s)
        return s

    def close(self):
        nums = [s.num for s in self.sems]
        self.nc.all_engine_barrier(sems_to_clear=range(min(nums), max(nums) + 1))
        self.ctx.close()


def in_pairs(eng, pairs, body):
    body(0, False)
    with eng.Fori(1, pairs - 1) as i:
        body(i, False)
    body(pairs - 1, True)


def pipelined(eng, tiles, plan):
    first = max(0, -min(ahead for _, ahead in plan))
    deep = max(0, max(ahead for _, ahead in plan))

    def step(i, off):
        for stage, ahead in plan:
            if not isinstance(i, int):
                stage((i, off + ahead))
            elif 0 <= off + ahead < tiles:
                stage((0, off + ahead))
    begin = (first + 3) // 2
    end = (tiles - deep) // 2
    for t in range(-deep, 2 * begin):
        step(0, t)
    with eng.Fori(begin, end) as i:
        step(i, 0)
        step(i, 1)
    for t in range(2 * end, tiles + first):
        step(0, t)


def of(t, n, c=0):
    i, off = t
    return i * (2 * n) + (off * n + c)


def at(t, width=1):
    i, off = t
    if isinstance(i, int):
        return slice((2 * i + off) * width, (2 * i + off + 1) * width)
    return bass.ds(of(t, width), width)


def load_projection(sp, w, loaded, g_in, Wq, Wkv, null_bias, mask, scales=()):
    sp.dma_start(w["Wq"][:, :, :], Wq.rearrange("(k p) n -> p k n", p=P)).then_inc(loaded, 16)
    sp.dma_start(w["Wkv"][:, :, :], Wkv.rearrange("(k p) n -> p k n", p=P)).then_inc(loaded, 16)
    sp.dma_start(w["gcol"][:, :], g_in.rearrange("(k p) -> p k", p=P),
                 allow_slow_non_contiguous=True).then_inc(loaded, 16)
    sp.dma_start(w["nb"][:, :], row_of(null_bias, H)).then_inc(loaded, 16)
    sp.dma_start(w["mask8"][:, :].rearrange("p (b t) -> p b t", b=B), mask.rearrange("b (t p) -> p b t", p=P),
                 allow_slow_non_contiguous=True).then_inc(loaded, 16)
    for dst, src in zip(("qsr", "ksr"), scales):
        sp.dma_start(w[dst][:, :], row_of(src, DH)).then_inc(loaded, 16)


def load_output(sp, w, loaded, Wout, g_out):
    sp.dma_start(w["Wout"][:, :, :], Wout.rearrange("(j p) n -> p j n", p=P)).then_inc(loaded, 16)
    sp.dma_start(w["g_out"][:, :], row_of(g_out, D)).then_inc(loaded, 16)


def write_table(sp, table, shifted, stored):
    for h in range(0, H, HEADS_AT_ONCE):
        n = HEADS_AT_ONCE
        src = table[h:h + n, 0:PITCH - 1].unsqueeze(1).to_broadcast([n, P, PITCH - 1])
        dst = bass.AP(tensor=shifted.tensor, offset=shifted.offset + h * (P + 1) * PITCH,
                      ap=[[(P + 1) * PITCH, n], [PITCH + 1, P], [1, PITCH - 1]])
        sp.dma_start(dst, src).then_inc(stored, 16)


def bias_tables(nc, keep, x_tiles, layers, shifted, stored, load_next):
    sc = Scope(nc, "tables")
    sb, ps, sem = sc.sb, sc.ps, sc.sem
    NP = S // P
    NL = len(layers)
    rows = [[sb(f"{n}{l}", [P, D]) for n in ("w0r", "b0r", "g0r", "b1r", "g1r")] for l in range(NL)]
    w1s = [sb(f"w1s{l}", [P, KD, D]) for l in range(NL)]
    w2s = [sb(f"w2s{l}", [P, KD, H]) for l in range(NL)]
    b2c = [sb(f"b2c{l}", [H, 1]) for l in range(NL)]
    dist_i = sb("dist_i", [P, NP], I32)
    dist = sb("dist", [P, NP])
    eps = sb("eps", [P, 1])
    raw = [sb(f"raw{l}", [P, NP, D]) for l in range(NL)]
    act = [sb(f"act{l}", [P, NP, D]) for l in range(NL)]
    hT = [sb(f"hT{l}", [P, KD, S]) for l in range(NL)]
    stat = [sb(f"stat{l}", [P, NP, 6]) for l in range(NL)]
    mv = [sb(f"mv{l}", [P, NP, 2]) for l in range(NL)]
    std = [sb(f"std{l}", [P, NP]) for l in range(NL)]
    rstd = [sb(f"rstd{l}", [P, NP]) for l in range(NL)]
    t_ps = ps("t_ps", [P, 2, ONE_BANK])
    m_ps = ps("m_ps", [P, 2, ONE_BANK])
    b_ps = [ps(f"b_ps{l}", [H, S]) for l in range(NL)]
    ident, table = keep["ident"], keep["table"]
    (dist_made, eps_made, dve, var_ready, std_ready, normed, act_ready, turned, taken, product, h_taken,
     b_product, tab, x_in, zeroed) = (
        sem(n) for n in ("dist_made", "eps_made", "dve", "var_ready", "std_ready", "normed", "act_ready", "turned",
                         "taken", "product", "h_taken", "b_product", "tab", "x_in", "zeroed"))
    loaded = [sem(f"loaded{l}") for l in range(NL)]

    with nc.Block() as block:
        @block.sync
        def _(sp):
            for l, (w0, b0, g0, w1, b1, g1, w2, b2) in enumerate(layers):
                for dst, src in zip(rows[l], (w0, b0, g0, b1, g1)):
                    sp.dma_start(dst[:, :], row_of(src, D)).then_inc(loaded[l], 16)
                sp.dma_start(w1s[l][:, :, :], w1.rearrange("(k p) n -> p k n", p=P)).then_inc(loaded[l], 16)
                sp.dma_start(w2s[l][:, :, :], w2.rearrange("(k p) n -> p k n", p=P)).then_inc(loaded[l], 16)
                sp.dma_start(b2c[l][:, :], b2.rearrange("(h a) -> h a", a=1)).then_inc(loaded[l], 16)
            sp.dma_start(keep["X"][:, :, :], x_tiles).then_inc(x_in, 16)
            load_next(sp)
            sp.wait_ge(tab, NL + 2)
            write_table(sp, table[0], shifted[0], stored[0])
            sp.wait_ge(x_in, 16)

        @block.gpsimd
        def _(pool):
            pool.iota(dist_i[:, :], [[-P, NP]], base=S - 1, channel_multiplier=-1).then_inc(dist_made, 1)
            pool.memset(ident[:, :], 0.0).then_inc(zeroed, 1)
            pool.wait_ge(zeroed, 1)
            pool.affine_select(out=ident[:, :], in_=ident[:, :], compare_op=ALU.not_equal,
                               fill=1.0, base=0, pattern=[[-1, P]], channel_multiplier=1).then_inc(zeroed, 1)

        @block.vector
        def _(v):
            done = [0]

            def link(ins):
                done[0] += 1
                ins.then_inc(dve, 1)
                v.wait_ge(dve, done[0])

            def stats(l):
                for q in range(NP):
                    last = v.bn_stats(stat[l][:, q, :], raw[l][:, q, :])
                link(last)
                for q in range(NP):
                    last = v.bn_aggr(mv[l][:, q, :], stat[l][:, q, :])
                last.then_inc(var_ready, 1)

            def norm(l, which):
                v.wait_ge(std_ready, which * NL + l + 1)
                link(v.reciprocal(rstd[l][:, :], std[l][:, :]))
                for q in range(NP):
                    last = v.tensor_scalar(raw[l][:, q, :], raw[l][:, q, :], mv[l][:, q, 0:1], rstd[l][:, q:q + 1],
                                           ALU.subtract, ALU.mult)
                link(last)
                gain = rows[l][4 if which else 2]
                v.tensor_tensor(act[l][:, :, :], raw[l][:, :, :], repeat(gain[:, :], NP), ALU.mult).then_inc(normed, 1)

            v.memset(eps[:, :], EPS).then_inc(eps_made, 1)
            for l in range(NL):
                v.memset(table[l][:, S:PITCH], BIG).then_inc(tab, 1)
            v.wait_ge(dist_made, 1)
            link(v.tensor_copy(dist[:, :], dist_i[:, :]))
            for l in range(NL):
                w0r, b0r = rows[l][0:2]
                v.wait_ge(loaded[l], 16 * 8)
                for q in range(NP):
                    last = v.scalar_tensor_tensor(out=raw[l][:, q, :], in0=w0r[:, :], scalar=dist[:, q:q + 1],
                                                  in1=b0r[:, :], op0=ALU.mult, op1=ALU.add)
                link(last)
                stats(l)
            for l in range(NL):
                norm(l, 0)
            for l in range(NL):
                for q in range(NP):
                    n = l * NP + q
                    v.wait_ge(product, n + 1)
                    v.tensor_tensor(raw[l][:, q, :], m_ps[:, n % 2, 0:D], rows[l][3][:, :], ALU.add).then_inc(h_taken, 1)
                v.wait_ge(h_taken, (l + 1) * NP)
                stats(l)
                if l:
                    norm(l - 1, 1)
            norm(NL - 1, 1)
            for l in range(NL):
                for c in range(2):
                    v.wait_ge(b_product, 2 * l + c + 1)
                    v.tensor_scalar(table[l][:, c * ONE_BANK:(c + 1) * ONE_BANK],
                                    b_ps[l][:, c * ONE_BANK:(c + 1) * ONE_BANK], b2c[l][:, :], -1.0,
                                    ALU.add, ALU.mult).then_inc(tab, 1)

        @block.scalar
        def _(a):
            def root(l, which):
                a.wait_ge(var_ready, which * NL + l + 1)
                a.activation(std[l][:, :], mv[l][:, :, 1], ACT.Sqrt, bias=eps[:, :]).then_inc(std_ready, 1)

            def silu(l, which):
                a.wait_ge(normed, which * NL + l + 1)
                a.activation(act[l][:, :, :], act[l][:, :, :], ACT.Silu).then_inc(act_ready, 1)

            def take(l, which):
                for q in range(NP):
                    n = (which * NL + l) * NP + q
                    a.wait_ge(turned, n + 1)
                    if which and q == 0:
                        a.wait_ge(product, (l + 1) * NP)
                    a.activation(hT[l][:, :, q * P:(q + 1) * P],
                                 t_ps[:, n % 2, 0:KD * P].rearrange("p (k n) -> p k n", k=KD),
                                 ACT.Copy).then_inc(taken, 1)

            a.wait_ge(eps_made, 1)
            for l in range(NL):
                root(l, 0)
            for l in range(NL):
                silu(l, 0)
                take(l, 0)
            for l in range(NL):
                root(l, 1)
            for l in range(NL):
                silu(l, 1)
                take(l, 1)

        @block.tensor
        def _(pe):
            def turn(l, which, q):
                n = (which * NL + l) * NP + q
                wait(pe, taken, n - 1)
                for k in range(KD):
                    last = pe.transpose(t_ps[:, n % 2, k * P:(k + 1) * P],
                                        act[l][:, q, k * P:(k + 1) * P], ident[:, :])
                last.then_inc(turned, 1)

            def product_of(l, q):
                n = l * NP + q
                pe.wait_ge(taken, n + 1)
                wait(pe, h_taken, n - 1)
                for k in range(KD):
                    last = pe.matmul(m_ps[:, n % 2, 0:D], hT[l][:, k, q * P:(q + 1) * P],
                                     w1s[l][:, k, :], start=k == 0, stop=k == KD - 1)
                last.then_inc(product, 1)

            pe.wait_ge(zeroed, 2)
            for l in range(NL):
                pe.wait_ge(loaded[l], 16 * 8)
                pe.wait_ge(act_ready, l + 1)
                turn(l, 0, 0)
                for q in range(NP):
                    if q + 1 < NP:
                        turn(l, 0, q + 1)
                    product_of(l, q)
            for l in range(NL):
                pe.wait_ge(act_ready, NL + l + 1)
                for q in range(NP):
                    turn(l, 1, q)
                pe.wait_ge(taken, (NL + l + 1) * NP)
                for c in range(2):
                    for k in range(KD):
                        last = pe.matmul(b_ps[l][:, c * ONE_BANK:(c + 1) * ONE_BANK], w2s[l][:, k, :],
                                         hT[l][:, k, c * ONE_BANK:(c + 1) * ONE_BANK],
                                         start=k == 0, stop=k == KD - 1)
                    last.then_inc(b_product, 1)
    sc.close()


def project(nc, keep, tag, cosine, loaded, qT_dram, wait_tables=None):
    sc = Scope(nc, tag)
    sb, ps, sem = sc.sb, sc.ps, sc.sem
    ident, X, K1, K2, V, NS = (keep[n] for n in ("ident", "X", "K1", "K2", "V", "NS"))
    v_raw = sb("v_raw", [P, NT, DH])
    v_scaled = sb("v_scaled", [P, NT, DH])
    vmx = sb("vmx", [P, 4])
    vtop = sb("vtop", [1, 2])
    ones = sb("ones", [1, P])
    sign = -1.0 if cosine else 1.0
    factor = -8.0 if cosine else DH ** -0.5
    HK = H + 1
    W, Wk, gcol, qsr, ksr, nk, nb, mask8 = (
        keep["w"][n] for n in ("Wq", "Wkv", "gcol", "qsr", "ksr", "null_key", "nb", "mask8"))
    kf = sb("kf", [P, DH])
    nksq = sb("nksq", [P, DH])
    nks = sb("nks", [P, 4])
    nkf = sb("nkf", [P, DH])
    maskf = sb("maskf", [P, NT])
    eps = sb("eps", [P, 1])
    stat = sb("stat", [P, NT, 6])
    mv = sb("mv", [P, NT, 2])
    std = sb("std", [P, NT])
    rstd = sb("rstd", [P, NT])
    xn = sb("xn", [P, 2, D])
    xT = sb("xT", [P, 2, KD, P])
    qs = sb("qs", [P, 2, HK, DH])
    sq = sb("sq", [P, HK, DH])
    ss = sb("ss", [P, HK])
    nrm = sb("nrm", [P, HK])
    rn = sb("rn", [P, HK])
    qn = sb("qn", [P, 2, HK, DH]) if cosine else qs
    kn = sb("kn", [P, 2, DH])
    nprod = sb("nprod", [P, 2, H, DH])
    nsum = sb("nsum", [P, H])
    QR = sb("QR", [P, 2, H + 2, P], F32R)
    QRf = QR[:, :, :, :].bitcast(F32)
    qTs = sb("qTs", [P, 2, H, P])
    x_ps = ps("x_ps", [P, ONE_BANK])
    q_ps = ps("q_ps", [P, H * DH])
    kv_ps = ps("kv_ps", [P, ONE_BANK])
    tr_ps = ps("tr_ps", [P, 2, ONE_BANK])
    (w_ready, var_ready, std_ready, null_sq, null_std, dve0, eps_ready, rstd_ready) = (
        sem(n) for n in ("w_ready", "var_ready", "std_ready", "null_sq", "null_std", "dve0",
                         "eps_ready", "rstd_ready"))
    (xn_ready, x_turned, xT_ready, q_product, q_taken, sq_ready, ss_ready, nrm_ready, qn_ready,
     kn_ready, null_prod, q_hi, k_hi, q_lo, null_sum, null_done, chain) = (
        sem(n) for n in ("xn_ready", "x_turned", "xT_ready", "q_product", "q_taken",
                         "sq_ready", "ss_ready", "nrm_ready", "qn_ready", "kn_ready", "null_prod",
                         "q_hi", "k_hi", "q_lo", "null_sum", "null_done", "chain"))
    turned = [sem("turned0"), sem("turned1")]
    emptied = [sem("emptied0"), sem("emptied1")]
    v_max, v_turned, v_top, v_spread, v_hi = (
        sem(n) for n in ("v_max", "v_turned", "v_top", "v_spread", "v_hi"))
    q_stored = [sem("q_stored0"), sem("q_stored1")]
    LOADS = 7 if cosine else 5
    per = [3, 2]

    with nc.Block() as block:
        @block.sync
        def _(sp):
            def store(t):
                par = t[1] % 2
                wait_alone(sp, emptied[0], of(t, per[0], 2))
                wait_alone(sp, emptied[1], of(t, per[1], 2))
                sp.dma_start(qT_dram[:, :, at(t, P)].rearrange("h p n -> p h n"),
                             qTs[:, par, :, :]).then_inc(q_stored[par], 16)
            pipelined(sp, NT, [(store, 0)])
            if wait_tables is not None:
                sp.wait_ge(wait_tables, 16 * H // HEADS_AT_ONCE)
            for off in range(2):
                sp.wait_ge(q_stored[off], 16 * (NT // 2))

        @block.gpsimd
        def _(pool):
            pool.wait_ge(w_ready, 1)

            def null_and_k(t):
                par = t[1] % 2
                wait(pool, qn_ready if cosine else q_taken, of(t, 1, 1))
                wait(pool, q_lo, of(t, 1, -1))
                pool.tensor_tensor(kn[:, par, :], qn[:, par, H, :], kf[:, :], ALU.mult).then_inc(kn_ready, 1)
                wait(pool, null_done, of(t, 1, -1))
                pool.tensor_tensor(nprod[:, par, :, :], qn[:, par, 0:H, :], repeat(nkf[:, :], H),
                                   ALU.mult).then_inc(null_prod, 1)
            pipelined(pool, NT, [(null_and_k, 1)])

        @block.vector
        def _(v):
            done = [0]

            def link(ins):
                done[0] += 1
                ins.then_inc(dve0, 1)
                v.wait_ge(dve0, done[0])

            v.memset(eps[:, :], EPS).then_inc(eps_ready, 1)
            for t in range(NT):
                last = v.bn_stats(stat[:, t, :], X[:, t, :])
            link(last)
            for t in range(NT):
                last = v.bn_aggr(mv[:, t, :], stat[:, t, :])
            last.then_inc(var_ready, 1)
            v.wait_ge(loaded, 16 * LOADS)
            v.wait_ge(keep["null_in"], 32)
            if cosine:
                link(v.tensor_tensor(nksq[:, :], nk[:, :], nk[:, :], ALU.mult))
                v.tensor_reduce(nks[:, 0:1], nksq[:, :], AX_X, ALU.add).then_inc(null_sq, 1)
                link(v.tensor_tensor(kf[:, :], qsr[:, :], ksr[:, :], ALU.mult))
                link(v.tensor_scalar(kf[:, :], kf[:, :], factor, None, ALU.mult))
            else:
                link(v.memset(kf[:, :], factor))
            for k in range(KD):
                v.tensor_scalar(W[:, k, :], W[:, k, :], gcol[:, k:k + 1], None, ALU.mult)
                last = v.tensor_scalar(Wk[:, k, :], Wk[:, k, :], gcol[:, k:k + 1], None, ALU.mult)
            link(last)
            link(v.tensor_scalar(nb[:, :], nb[:, :], -1.0, None, ALU.mult))
            link(v.tensor_copy(maskf[:, :], mask8[:, :]))
            link(v.tensor_scalar(maskf[:, :], maskf[:, :], sign * BIG, -sign * BIG, ALU.mult, ALU.add))
            if cosine:
                v.wait_ge(null_std, 1)
                link(v.tensor_scalar(nks[:, 2:3], nks[:, 1:2], 1e-12, None, ALU.max))
                link(v.reciprocal(nks[:, 3:4], nks[:, 2:3]))
                link(v.tensor_scalar(nksq[:, :], nk[:, :], nks[:, 3:4], None, ALU.mult))
                v.tensor_tensor(nkf[:, :], nksq[:, :], kf[:, :], ALU.mult).then_inc(w_ready, 1)
            else:
                link(v.tensor_scalar(nksq[:, :], nk[:, :], -1.0, None, ALU.mult))
                v.tensor_tensor(nkf[:, :], nksq[:, :], kf[:, :], ALU.mult).then_inc(w_ready, 1)
            v.wait_ge(std_ready, 1)
            v.reciprocal(rstd[:, :], std[:, :]).then_inc(rstd_ready, 1)
            v.wait_ge(rstd_ready, 1)

            def normalise(t):
                par = t[1] % 2
                wait(v, x_turned, of(t, 1, -1))
                v.tensor_scalar(xn[:, par, :], X[:, at(t), :].rearrange("p a n -> p (a n)"), mv[:, at(t), 0],
                                rstd[:, at(t)], ALU.subtract, ALU.mult).then_inc(xn_ready, 1)

            def norms(t):
                wait(v, sq_ready, of(t, 1, 1))
                v.tensor_reduce(ss[:, :], sq[:, :, :], AX_X, ALU.add).then_inc(ss_ready, 1)

            def scale(t):
                par = t[1] % 2
                wait(v, nrm_ready, of(t, 1, 1))
                v.tensor_scalar(rn[:, :], nrm[:, :], 1e-12, None, ALU.max).then_inc(chain, 1)
                wait(v, chain, of(t, 2, 1))
                v.reciprocal(rn[:, :], rn[:, :]).then_inc(chain, 1)
                wait(v, chain, of(t, 2, 2))
                wait(v, k_hi, of(t, 1, -1))
                wait(v, null_prod, of(t, 1, -1))
                v.tensor_tensor(qn[:, par, :, :], qs[:, par, :, :], spread(rn[:, :], DH),
                                ALU.mult).then_inc(qn_ready, 1)

            def low_halves(t):
                par = t[1] % 2
                wait(v, q_hi, of(t, 1, 1))
                v.tensor_tensor(QR[:, par, 0:H, DH:P], qn[:, par, 0:H, :], QRf[:, par, 0:H, 0:DH], ALU.subtract)
                v.tensor_copy(QR[:, par, H + 1, DH:DH + 1], maskf[:, at(t)])
                wait(v, k_hi, of(t, 1, 1))
                v.tensor_tensor(QR[:, par, H + 1, 0:DH], kn[:, par, :], QRf[:, par, H, 0:DH],
                                ALU.subtract).then_inc(q_lo, 1)

            def empty(t, j):
                par, g = t[1] % 2, 2 * j + 1
                wait(v, turned[1], of(t, per[1], j + 1))
                if j == 0:
                    wait(v, q_stored[par], t[0] * 16 + t[1] // 2 * 16)
                v.tensor_copy(qTs[:, par, 4 * g:4 * g + 4, :],
                              tr_ps[:, 1, :].rearrange("p (a n) -> p a n", a=4)).then_inc(emptied[1], 1)

            def null_scores(t):
                wait(v, null_prod, of(t, 1, 1))
                v.tensor_reduce(nsum[:, :], nprod[:, t[1] % 2, :, :], AX_X, ALU.add).then_inc(null_sum, 1)
                wait(v, null_sum, of(t, 1, 1))
                v.tensor_tensor(NS[:, :, at(t)], nsum[:, :].unsqueeze(2), nb[:, :].unsqueeze(2),
                                ALU.add).then_inc(null_done, 1)

            first, second = (lambda t: empty(t, 0), 0), (lambda t: empty(t, 1), 0)
            pipelined(v, NT, [(normalise, 4), (low_halves, 0), (norms, 1), first, (scale, 1), (null_scores, 0), second] if cosine else
                      [(normalise, 4), (low_halves, 0), first, (null_scores, 0), second])
            v.wait_ge(q_taken, NT)
            link(v.tensor_reduce(vmx[:, 0:1], v_raw[:, :, :], AX_XY, ALU.max))
            link(v.tensor_reduce(vmx[:, 1:2], v_raw[:, :, :], AX_XY, ALU.min))
            link(v.tensor_scalar(vmx[:, 2:3], vmx[:, 1:2], -1.0, None, ALU.mult))
            v.tensor_tensor(vmx[:, 3:4], vmx[:, 0:1], vmx[:, 2:3], ALU.max).then_inc(v_max, 1)
            v.memset(ones[:, :], 1.0).then_inc(v_max, 1)
            v.wait_ge(v_turned, 1)
            link(v.tensor_reduce(vtop[:, 0:1], x_ps[0:1, 0:P], AX_X, ALU.max))
            v.tensor_scalar(vtop[:, 1:2], vtop[:, 0:1], 1e-30, None, ALU.max).then_inc(v_top, 1)
            v.wait_ge(v_spread, 1)
            link(v.tensor_scalar(keep["v_back"][:, :], x_ps[:, P:P + 1], 1.0 / (P_SCALE * V_SCALE), None, ALU.mult))
            link(v.reciprocal(vmx[:, 0:1], x_ps[:, P:P + 1]))
            link(v.tensor_scalar(v_scaled[:, :, :], v_raw[:, :, :], vmx[:, 0:1], V_SCALE, ALU.mult, ALU.mult))
            link(v.tensor_copy(V[:, :, 0:DH], v_scaled[:, :, :]))
            v.tensor_tensor(V[:, :, DH:2 * DH], v_scaled[:, :, :], V[:, :, 0:DH], ALU.subtract).then_inc(v_hi, 1)

        @block.scalar
        def _(a):
            a.wait_ge(eps_ready, 1)
            a.wait_ge(var_ready, 1)
            a.activation(std[:, :], mv[:, :, 1], ACT.Sqrt, bias=eps[:, :]).then_inc(std_ready, 1)
            if cosine:
                a.wait_ge(null_sq, 1)
                a.activation(nks[:, 1:2], nks[:, 0:1], ACT.Sqrt).then_inc(null_std, 1)

            def take_x(t):
                wait(a, x_turned, of(t, 1, 1))
                wait(a, q_product, of(t, 1, -1))
                a.activation(xT[:, t[1] % 2, :, :], x_ps[:, 0:KD * P].rearrange("p (k n) -> p k n", k=KD),
                             ACT.Copy).then_inc(xT_ready, 1)

            def take_qkv(t):
                par = t[1] % 2
                wait(a, q_product, of(t, 1, 1))
                if cosine:
                    wait(a, qn_ready, of(t, 1, -1))
                else:
                    wait(a, q_lo, of(t, 1, -1))
                    wait(a, null_prod, of(t, 1, -1))
                a.activation(qs[:, par, 0:H, :], q_ps[:, :].rearrange("p (h n) -> p h n", h=H), ACT.Copy)
                a.activation(qs[:, par, H, :], kv_ps[:, 0:DH], ACT.Copy)
                a.activation(v_raw[:, at(t), :], kv_ps[:, DH:2 * DH].unsqueeze(1), ACT.Copy).then_inc(q_taken, 1)

            def squares(t):
                wait(a, q_taken, of(t, 1, 1))
                wait(a, ss_ready, of(t, 1))
                a.activation(sq[:, :, :], qs[:, t[1] % 2, :, :], ACT.Square).then_inc(sq_ready, 1)

            def roots(t):
                wait(a, ss_ready, of(t, 1, 1))
                wait(a, qn_ready, of(t, 1))
                a.activation(nrm[:, :], ss[:, :], ACT.Sqrt).then_inc(nrm_ready, 1)

            def high_halves(t):
                par = t[1] % 2
                wait(a, qn_ready if cosine else q_taken, of(t, 1, 1))
                wait(a, turned[0], of(t, per[0], -per[0]))
                wait(a, turned[1], of(t, per[1], -per[1]))
                a.activation(QR[:, par, 0:H, 0:DH], qn[:, par, 0:H, :], ACT.Copy).then_inc(q_hi, 1)
                wait(a, kn_ready, of(t, 1, 1))
                a.activation(QR[:, par, H, 0:DH], kn[:, par, :], ACT.Copy)
                a.activation(QR[:, par, H, DH:P], kn[:, par, :], ACT.Copy).then_inc(k_hi, 1)

            def empty(t):
                par = t[1] % 2
                for j, g in enumerate((0, 2)):
                    wait(a, turned[0], of(t, per[0], j + 1))
                    if j == 0:
                        wait(a, q_stored[par], t[0] * 16 + t[1] // 2 * 16)
                    a.activation(qTs[:, par, 4 * g:4 * g + 4, :], tr_ps[:, 0, :].rearrange("p (a n) -> p a n", a=4),
                                 ACT.Copy).then_inc(emptied[0], 1)
                wait(a, turned[0], of(t, per[0], 3))
                a.activation(K1[:, at(t, P)], tr_ps[:, 0, 0:P], ACT.Copy)
                a.activation(K2[:, at(t, P)], tr_ps[0:DH + 1, 0, P:2 * P], ACT.Copy).then_inc(emptied[0], 1)

            if cosine:
                pipelined(a, NT, [(take_x, 3), (high_halves, 0), (squares, 1), (take_qkv, 2), (roots, 1), (empty, 0)])
            else:
                pipelined(a, NT, [(take_x, 3), (high_halves, 0), (take_qkv, 2), (empty, 0)])

        @block.tensor
        def _(pe):
            pe.wait_ge(w_ready, 1)

            def turn_x(t):
                par = t[1] % 2
                wait(pe, xn_ready, of(t, 1, 1))
                wait(pe, xT_ready, of(t, 1))
                for k in range(KD):
                    last = pe.transpose(x_ps[:, k * P:(k + 1) * P], xn[:, par, k * P:(k + 1) * P], ident[:, :])
                last.then_inc(x_turned, 1)

            def products(t):
                par = t[1] % 2
                wait(pe, xT_ready, of(t, 1, 1))
                wait(pe, q_taken, of(t, 1))
                for c in range(H * DH // ONE_BANK):
                    cols = slice(c * ONE_BANK, (c + 1) * ONE_BANK)
                    for k in range(KD):
                        pe.matmul(q_ps[:, cols], xT[:, par, k, :], W[:, k, cols], start=k == 0, stop=k == KD - 1)
                for k in range(KD):
                    last = pe.matmul(kv_ps[:, 0:2 * DH], xT[:, par, k, :], Wk[:, k, :], start=k == 0, stop=k == KD - 1)
                last.then_inc(q_product, 1)

            def turn_qk(t):
                par = t[1] % 2
                wait(pe, q_lo, of(t, 1, 1))
                for g in range(5):
                    bank, j = g % 2, g // 2
                    wait(pe, emptied[bank], of(t, per[bank], j))
                    for n in range(4 * g, min(4 * g + 4, H + 1)):
                        last = pe.transpose(tr_ps[:, bank, (n - 4 * g) * P:(n - 4 * g + 1) * P],
                                            QRf[:, par, n, :], ident[:, :])
                    if g == 4:
                        last = pe.transpose(tr_ps[0:DH + 1, bank, P:2 * P], QRf[:, par, H + 1, 0:DH + 1], ident[:, :])
                    last.then_inc(turned[bank], 1)

            pipelined(pe, NT, [(turn_x, 3), (products, 2), (turn_qk, 0)])
            pe.wait_ge(v_max, 2)
            pe.transpose(x_ps[0:1, 0:P], vmx[:, 3:4], ident[:, :]).then_inc(v_turned, 1)
            pe.wait_ge(v_top, 1)
            pe.matmul(x_ps[:, P:P + 1], ones[:, :], vtop[:, 1:2], start=True, stop=True).then_inc(v_spread, 1)
    sc.close()


def attend(nc, keep, tag, cosine, bias, qT_dram, o_dram, load_next):
    sc = Scope(nc, tag)
    sb, ps, sem = sc.sb, sc.ps, sc.sem
    ident, K1, K2, V, NS, NV = (keep[n] for n in ("ident", "K1", "K2", "V", "NS", "NV"))
    RING = 6
    TURNS, SUMS = 3, 1
    q1 = [sb(f"q1_{b}", [P, S], F32R) for b in range(B)]
    q2 = [sb(f"q2_{b}", [DH + 1, S], F32R) for b in range(B)]
    width = S if cosine else TRI * P
    bias_sb = [sb(f"bias_{n}", [P, width]) for n in range(2)]
    prob = [sb(f"prob_{n}", [P, TRI * P]) for n in range(2)]
    pT_hi = [sb(f"pT_hi{n}", [P, ONE_BANK], F16) for n in range(RING)]
    pT_lo = [sb(f"pT_lo{n}", [P, ONE_BANK], F16) for n in range(RING)]
    nsu = [sb(f"nsu{n}", [P, RT]) for n in range(2)]
    ext = [sb(f"ext{n}", [P, RT]) for n in range(2)]
    rsum = [sb(f"rsum{n}", [P, RT]) for n in range(2)]
    nexp = [sb(f"nexp{n}", [P, RT]) for n in range(2)]
    nprob = [sb(f"nprob{n}", [P, RT]) for n in range(2)]
    den = [sb(f"den{n}", [P, RT]) for n in range(2)]
    rden = [sb(f"rden{n}", [P, RT]) for n in range(2)]
    rback = [sb(f"rback{n}", [P, RT]) for n in range(2)]
    back_ready = sem("back_ready")
    nw = [sb(f"nw{n}", [P, RT]) for n in range(2)]
    o_null = sb("o_null", [P, RT, DH])
    o_sb = [sb(f"o_sb{n}", [P, RT, DH]) for n in range(2)]
    s_ps = [ps(f"s_ps{n}", [P, S]) for n in range(2)]
    t_ps = [ps(f"t_ps{n}", [P, ONE_BANK]) for n in range(TURNS)]
    o_ps = [ps(f"o_ps{n}", [P, RT, DH]) for n in range(SUMS)]
    q_in = [sem(f"q_in{b}") for b in range(B)]
    bias_in = [sem(f"bias_in{n}") for n in range(2)]
    (scored, row_added, exp_done, turned, hi_ready, lo_ready, pv_done, null_in, null_diff, null_exp,
     den_ready, rden_ready, o_taken, o_scaled, null_weight, null_value, o_ready, ones_ready) = (
        sem(n) for n in ("scored", "row_added", "exp_done", "turned", "hi_ready", "lo_ready", "pv_done",
                         "null_in", "null_diff", "null_exp", "den_ready", "rden_ready", "o_taken",
                         "o_scaled", "null_weight", "null_value", "o_ready", "ones_ready"))
    o_stored = [sem("o_stored0"), sem("o_stored1")]
    bias_masked = [sem(f"bias_masked{n}") for n in range(2)]
    order = [x for r in (3, 1, 0, 2) for x in (r, RT - 1 - r)]
    start = [sum(r + 1 for r in order[:p]) for p in range(RT + 1)]
    tiles = [(r, c) for r in order for c in range(r + 1)]
    done_after = [start[p + 1] // 4 for p in range(RT)]
    first_of = [0] + done_after[:-1]
    LAG = 2

    def g_slot(off, g):
        assert 4 * GROUPS % RING == 0
        return (GROUPS * off + g) % RING

    def count(u, n, c=0):
        i, off = u
        return i * (4 * n) + (off * n + c)

    def ahead(u, p, by):
        i, off = u
        return (i, off + (p + by) // RT), (p + by) % RT

    def in_steps(eng, step):
        def body(i, last):
            for off in range(4):
                for p in range(RT):
                    step((i, off), p, (RT * (4 - off) - p) if last else 99)
        in_pairs(eng, H // 2, body)

    with nc.Block() as block:
        @block.sync
        def _(sp):
            def load_bias(u):
                i, off = u
                head = i * 2 + off // 2
                buf = (off // 2) % 2
                wait_alone(sp, row_added, count(u, RT, -2 * RT))
                hs = bass.ds(head, 1) if not isinstance(head, int) else slice(head, head + 1)
                if cosine:
                    src = bias[hs, 0:P, P - 1:P - 1 + S].rearrange("a p n -> p (a n)")
                    sp.dma_start(bias_sb[buf][:, :], src).then_inc(bias_in[buf], 16)
                else:
                    for r in range(RT):
                        src = bias[hs, r * P:(r + 1) * P, 0:(r + 1) * P].rearrange("a p n -> p (a n)")
                        at = r * (r + 1) // 2 * P
                        sp.dma_start(bias_sb[buf][:, at:at + (r + 1) * P], src).then_inc(bias_in[buf], 16)

            def load_q(u):
                i, off = u
                head = i * 2 + off // 2
                b = off % 2
                wait_alone(sp, scored, count(u, RT, -RT))
                hs = bass.ds(head, 1) if not isinstance(head, int) else slice(head, head + 1)
                src = qT_dram[hs, :, b * S:(b + 1) * S]
                sp.dma_start(q1[b][:, :].bitcast(F32), src.rearrange("a p n -> p (a n)")).then_inc(q_in[b], 16)
                sp.dma_start(q2[b][0:DH, :].bitcast(F32), src[:, 0:DH, :].rearrange("a p n -> p (a n)")).then_inc(q_in[b], 16)

            def body(i, last):
                for off in range(4):
                    u = (i, off)
                    if off % 2 == 0 and not (last and off == 2):
                        load_bias((i, off + 2))
                    if not (last and off >= 2):
                        load_q((i, off + 2))
                    wait_alone(sp, o_ready, count(u, 1, 1))
                    head, b = i * 2 + off // 2, off % 2
                    cols = bass.ds(head * DH, DH) if not isinstance(head, int) else slice(head * DH, (head + 1) * DH)
                    sp.dma_start(o_dram[b * RT:(b + 1) * RT, :, cols].rearrange("t p n -> p t n"),
                                 o_sb[b][:, :, :]).then_inc(o_stored[b], 16)
            load_bias((0, 0))
            load_q((0, 0))
            load_q((0, 1))
            load_next(sp)
            in_pairs(sp, H // 2, body)
            for b in range(B):
                sp.wait_ge(o_stored[b], 16 * H)

        @block.tensor
        def _(pe):
            pe.wait_ge(ones_ready, 1)

            def scores(u, p):
                off = u[1]
                b, r = off % 2, order[p]
                if p == 0:
                    wait(pe, q_in[b], u[0] * 64 + (off // 2 + 1) * 32)
                wait(pe, row_added, count(u, RT, p - 1))
                n = (r + 1) * P
                for c in range(0, n, ONE_BANK):
                    w = min(ONE_BANK, n - c)
                    pe.matmul(s_ps[p % 2][:, c:c + w], q1[b][:, r * P:(r + 1) * P],
                              K1[:, b * S + c:b * S + c + w], start=True, stop=False)
                    last = pe.matmul(s_ps[p % 2][:, c:c + w], q2[b][:, r * P:(r + 1) * P],
                                     K2[:, b * S + c:b * S + c + w], start=False, stop=True)
                last.then_inc(scored, 1)

            def turn(u, p):
                i, off = u
                wait(pe, exp_done, count(u, RT, p + 1))
                for s in range(start[p], start[p + 1]):
                    g, j = divmod(s, 4)
                    bank = (GROUPS * off + g) % TURNS
                    if j == 0:
                        wait(pe, lo_ready, count(u, GROUPS, g + 1 - TURNS))
                    last = pe.transpose(t_ps[bank][:, j * P:(j + 1) * P], prob[off % 2][:, s * P:(s + 1) * P], ident[:, :])
                    if j == 3:
                        last.then_inc(turned, 1)
                        if g >= LAG:
                            weigh(u, g - LAG)
                        elif not very_first(u):
                            weigh((i, off - 1), GROUPS + g - LAG)

            def weigh(u, g):
                off = u[1]
                b = off % 2
                slot = g_slot(off, g)
                if g == 0:
                    wait(pe, o_taken, count(u, 1, 1 - SUMS))
                wait(pe, lo_ready, count(u, GROUPS, g + 1))
                for j in range(4):
                    r, c = tiles[4 * g + j]
                    sums = o_ps[off % SUMS][:, r, :]
                    hi, lo = pT_hi[slot][:, j * P:(j + 1) * P], pT_lo[slot][:, j * P:(j + 1) * P]
                    v_hi, v_lo = V[:, b * RT + c, 0:DH], V[:, b * RT + c, DH:2 * DH]
                    pe.matmul(sums, hi, v_hi, start=c == 0, stop=False)
                    pe.matmul(sums, hi, v_lo, start=False, stop=False)
                    last = pe.matmul(sums, lo, v_hi, start=False, stop=c == r)
                last.then_inc(pv_done, 1)

            def step(u, p, left):
                if left > 2:
                    scores(*ahead(u, p, 2))
                turn(u, p)
            scores((0, 0), 0)
            scores((0, 0), 1)
            in_steps(pe, step)
            for g in range(GROUPS - LAG, GROUPS):
                weigh((H // 2 - 1, 3), g)

        @block.vector
        def _(v):
            for b in range(B):
                last = v.memset(q2[b][DH:DH + 1, :].bitcast(F32), 1.0)
            last.then_inc(ones_ready, 1)

            def add(u, p):
                off = u[1]
                par, buf, r = off % 2, (off // 2) % 2, order[p]
                n = (r + 1) * P
                at = start[p] * P
                if p == 0:
                    wait(v, null_in, count(u, 1, 1))
                    if off % 2 == 0:
                        turn_of = u[0] + (off // 4 + 1)
                        if cosine:
                            wait(v, bias_in[buf], turn_of * 16)
                        else:
                            wait(v, bias_masked[buf], turn_of * RT)
                    wait(v, turned, count(u, GROUPS, -GROUPS))
                    wait(v, null_diff, count(u, 1, -1))
                wait_alone(v, scored, count(u, RT, p + 1))
                tri = r * (r + 1) // 2 * P
                src = bias_sb[buf][:, (RT - 1 - r) * P:S] if cosine else bias_sb[buf][:, tri:tri + n]
                v.tensor_tensor_reduce(out=prob[par][:, at:at + n], in0=s_ps[p % 2][:, 0:n], in1=src,
                                       scale=1.0 if cosine else -1.0, scalar=nsu[par][:, r:r + 1], op0=ALU.add,
                                       op1=ALU.min, accum_out=ext[par][:, r:r + 1]).then_inc(row_added, 1)

            def split(u, g):
                off = u[1]
                slot, bank = g_slot(off, g), (GROUPS * off + g) % TURNS
                wait(v, hi_ready, count(u, GROUPS, g + 1))
                wait(v, pv_done, count(u, GROUPS, g + 1 - RING))
                v.scalar_tensor_tensor(out=pT_lo[slot][:, :], in0=t_ps[bank][:, :], scalar=P_SCALE,
                                       in1=pT_hi[slot][:, :], op0=ALU.mult, op1=ALU.subtract).then_inc(lo_ready, 1)

            def finish(u):
                par = u[1] % 2
                wait(v, den_ready, count(u, 1, 1))
                v.reciprocal(rden[par][:, :], den[par][:, :]).then_inc(rden_ready, 1)

            def step(u, p, left):
                if left > 2:
                    add(*ahead(u, p, 2))
                for g in range(first_of[p], done_after[p]):
                    split(u, g)
                if p == 1 and not very_first(u):
                    finish((u[0], u[1] - 1))
            add((0, 0), 0)
            add((0, 0), 1)
            in_steps(v, step)
            finish((H // 2 - 1, 3))

        @block.scalar
        def _(a):
            def exps(u, p):
                par, r = u[1] % 2, order[p]
                at = start[p] * P
                n = (r + 1) * P
                if p == 0:
                    wait(a, den_ready, count(u, 1, -1))
                wait(a, row_added, count(u, RT, p + 1))
                a.activation(prob[par][:, at:at + n], prob[par][:, at:at + n], ACT.Exp,
                             bias=ext[par][:, r:r + 1], scale=-1.0,
                             accum_out=rsum[par][:, r:r + 1]).then_inc(exp_done, 1)

            def split(u, g):
                off = u[1]
                slot, bank = g_slot(off, g), (GROUPS * off + g) % TURNS
                wait(a, turned, count(u, GROUPS, g + 1))
                wait(a, pv_done, count(u, GROUPS, g + 1 - RING))
                a.activation(pT_hi[slot][:, :], t_ps[bank][:, :], ACT.Copy, scale=P_SCALE).then_inc(hi_ready, 1)

            def finish(u):
                par = u[1] % 2
                wait(a, null_diff, count(u, 1, 1))
                wait(a, null_weight, count(u, 1, -1))
                a.activation(nexp[par][:, :], nprob[par][:, :], ACT.Exp).then_inc(null_exp, 1)
                wait(a, pv_done, count(u, GROUPS, GROUPS))
                wait(a, o_stored[par], u[0] * 32 + (u[1] // 2) * 16)
                a.activation(o_sb[par][:, :, :], o_ps[u[1] % SUMS][:, :, :], ACT.Copy).then_inc(o_taken, 1)

            def step(u, p, left):
                if left > 1:
                    exps(*ahead(u, p, 1))
                for g in range(first_of[p], done_after[p]):
                    split(u, g)
                if p == 1 and not very_first(u):
                    finish((u[0], u[1] - 1))
            exps((0, 0), 0)
            in_steps(a, step)
            finish((H // 2 - 1, 3))

        @block.gpsimd
        def _(pool):
            def null_scores(u):
                i, off = u
                head, b = i * 2 + off // 2, off % 2
                wait(pool, row_added, count(u, RT, -RT))
                hs = bass.ds(head, 1) if not isinstance(head, int) else slice(head, head + 1)
                src = NS[:, hs, b * RT:(b + 1) * RT].rearrange("p a n -> p (a n)")
                pool.tensor_copy(nsu[off % 2][:, :], src).then_inc(null_in, 1)

            def mask_bias(u):
                i, off = u
                buf = (off // 2) % 2
                wait_alone(pool, bias_in[buf], i * (16 * RT) + (off // 4 + 1) * 16 * RT)
                for r in range(RT):
                    at = (r * (r + 1) // 2 + r) * P
                    tile = bias_sb[buf][:, at:at + P]
                    pool.affine_select(out=tile, in_=tile, compare_op=ALU.is_ge, fill=-BIG, base=0,
                                       pattern=[[-1, P]], channel_multiplier=1).then_inc(bias_masked[buf], 1)

            def body(i, last):
                for off in range(4):
                    u = (i, off)
                    par = off % 2
                    if not cosine and off % 2 and not (last and off == 3):
                        mask_bias((i, off + 1))
                    wait(pool, row_added, count(u, RT, RT))
                    wait(pool, null_exp, count(u, 1, -1))
                    pool.tensor_tensor(nprob[par][:, :], ext[par][:, :], nsu[par][:, :], ALU.subtract).then_inc(null_diff, 1)
                    if not (last and off >= 2):
                        wait(pool, null_diff, count(u, 1, 1))
                        null_scores((i, off + 2))
                    wait(pool, null_exp, count(u, 1, 1))
                    wait(pool, exp_done, count(u, RT, RT))
                    wait(pool, rden_ready, count(u, 1, -1))
                    pool.tensor_tensor(den[par][:, :], rsum[par][:, :], nexp[par][:, :], ALU.add).then_inc(den_ready, 1)
                    wait(pool, rden_ready, count(u, 1, 1))
                    pool.tensor_tensor(nw[par][:, :], nexp[par][:, :], rden[par][:, :], ALU.mult).then_inc(null_weight, 1)
                    pool.tensor_tensor(rback[par][:, :], rden[par][:, :], keep["v_back"][:, :].to_broadcast([P, RT]),
                                       ALU.mult).then_inc(back_ready, 1)
                    wait(pool, null_weight, count(u, 1, 1))
                    wait(pool, o_ready, count(u, 1))
                    pool.tensor_tensor(o_null[:, :, :], spread(nw[par][:, :], DH), repeat(NV[:, :], RT), ALU.mult).then_inc(null_value, 1)
                    wait(pool, o_taken, count(u, 1, 1))
                    wait(pool, back_ready, count(u, 1, 1))
                    pool.tensor_tensor(o_sb[par][:, :, :], o_sb[par][:, :, :], spread(rback[par][:, :], DH), ALU.mult).then_inc(o_scaled, 1)
                    wait(pool, null_value, count(u, 1, 1))
                    wait(pool, o_scaled, count(u, 1, 1))
                    pool.tensor_tensor(o_sb[par][:, :, :], o_sb[par][:, :, :], o_null[:, :, :], ALU.add).then_inc(o_ready, 1)
            if not cosine:
                mask_bias((0, 0))
            null_scores((0, 0))
            null_scores((0, 1))
            in_pairs(pool, H // 2, body)
    sc.close()


def merge(nc, keep, tag, loaded, o_dram, load_next, out_tiles=None):
    sc = Scope(nc, tag)
    sb, ps, sem = sc.sb, sc.ps, sc.sem
    ident, X = keep["ident"], keep["X"]
    JT = H * DH // P
    W, gr = keep["w"]["Wout"], keep["w"]["g_out"]
    eps = sb("eps", [P, 1])
    o = sb("o", [P, 2, H * DH])
    oT_hi = sb("oT_hi", [P, 2, JT, P], F32R)
    oT_lo = sb("oT_lo", [P, 2, JT, P], F32R)
    W_hi = sb("W_hi", [P, JT, D], F32R)
    W_lo = sb("W_lo", [P, JT, D], F32R)
    stat = sb("stat", [P, 6])
    mv = sb("mv", [P, 2, 2])
    std = sb("std", [P, 2])
    rstd = sb("rstd", [P, 1])
    y = sb("y", [P, D])
    yg = sb("yg", [P, D])
    t_ps = ps("t_ps", [P, 2, H * DH])
    y_ps = ps("y_ps", [P, 2, ONE_BANK])
    turned, hi_ready, lo_ready, w_hi, w_lo, product, stats, var_ready, std_ready, chain, added, eps_ready = (
        sem(n) for n in ("turned", "hi_ready", "lo_ready", "w_hi", "w_lo", "product", "stats", "var_ready",
                         "std_ready", "chain", "added", "eps_ready"))
    o_in = [sem("o_in0"), sem("o_in1")]
    x_out = sem("x_out")
    LINKS = 3
    STORED_TILES = 4

    with nc.Block() as block:
        @block.sync
        def _(sp):
            def load(t):
                par = t[1] % 2
                wait_alone(sp, turned, of(t, 1, -1))
                sp.dma_start(o[:, par, :], o_dram[at(t), :, :].rearrange("a p n -> p (a n)")).then_inc(o_in[par], 16)
            pipelined(sp, NT, [(load, 0)])
            load_next(sp)
            if out_tiles is not None:
                for first in range(0, NT, STORED_TILES):
                    tiles = slice(first, first + STORED_TILES)
                    sp.wait_ge(added, first + STORED_TILES)
                    sp.dma_start(out_tiles[:, tiles, :], X[:, tiles, :]).then_inc(x_out, 16)
                sp.wait_ge(x_out, 16 * (NT // STORED_TILES))

        @block.tensor
        def _(pe):
            def turn(t):
                par = t[1] % 2
                wait(pe, o_in[par], t[0] * 16 + (t[1] // 2 + 1) * 16)
                wait(pe, lo_ready, of(t, 1, -1))
                for j in range(JT):
                    last = pe.transpose(t_ps[:, par, j * P:(j + 1) * P], o[:, par, j * P:(j + 1) * P], ident[:, :])
                last.then_inc(turned, 1)

            def products(t):
                par = t[1] % 2
                wait(pe, lo_ready, of(t, 1, 1))
                if very_first(t):
                    pe.wait_ge(w_lo, 1)
                wait(pe, chain, of(t, LINKS, -2 * LINKS + 2))
                for j in range(JT):
                    pe.matmul(y_ps[:, par, 0:D], oT_hi[:, par, j, :], W_hi[:, j, :], start=j == 0, stop=False)
                    pe.matmul(y_ps[:, par, 0:D], oT_hi[:, par, j, :], W_lo[:, j, :], start=False, stop=False)
                    last = pe.matmul(y_ps[:, par, 0:D], oT_lo[:, par, j, :], W_hi[:, j, :], start=False, stop=j == JT - 1)
                last.then_inc(product, 1)
            pipelined(pe, NT, [(turn, 1), (products, 0)])

        @block.scalar
        def _(a):
            a.wait_ge(eps_ready, 1)
            a.wait_ge(loaded, 32)
            a.activation(W_hi[:, :, :], W[:, :, :], ACT.Copy).then_inc(w_hi, 1)

            def take(t):
                off = t[1] % 2
                wait(a, turned, of(t, 1, 1))
                wait(a, product, of(t, 1, -1))
                a.activation(oT_hi[:, off, :, :], t_ps[:, off, :].rearrange("p (j n) -> p j n", n=P),
                             ACT.Copy).then_inc(hi_ready, 1)

            def root(t):
                off = t[1] % 2
                wait(a, var_ready, of(t, 1, 1))
                a.activation(std[:, off:off + 1], mv[:, off, 1:2], ACT.Sqrt, bias=eps[:, :]).then_inc(std_ready, 1)

            pipelined(a, NT, [(take, 1), (root, -1)])

        @block.vector
        def _(v):
            v.memset(eps[:, :], EPS).then_inc(eps_ready, 1)
            v.wait_ge(w_hi, 1)
            v.tensor_tensor(W_lo[:, :, :], W[:, :, :], W_hi[:, :, :].bitcast(F32), ALU.subtract).then_inc(w_lo, 1)

            def take(t):
                off = t[1] % 2
                wait(v, hi_ready, of(t, 1, 1))
                wait(v, product, of(t, 1, -1))
                v.tensor_tensor(oT_lo[:, off, :, :], t_ps[:, off, :].rearrange("p (j n) -> p j n", n=P),
                                oT_hi[:, off, :, :].bitcast(F32), ALU.subtract).then_inc(lo_ready, 1)

            def variance(t):
                off = t[1] % 2
                wait(v, product, of(t, 1, 1))
                v.bn_stats(stat[:, :], y_ps[:, off, 0:D]).then_inc(stats, 1)
                wait_alone(v, stats, of(t, 1, 1))
                v.bn_aggr(mv[:, off, :], stat[:, :]).then_inc(var_ready, 1)

            def norm(t):
                off = t[1] % 2
                wait(v, std_ready, of(t, 1, 1))
                v.reciprocal(rstd[:, :], std[:, off:off + 1]).then_inc(chain, 1)
                wait(v, chain, of(t, LINKS, 1))
                v.tensor_scalar(y[:, :], y_ps[:, off, 0:D], mv[:, off, 0:1], rstd[:, :], ALU.subtract, ALU.mult).then_inc(chain, 1)
                wait(v, chain, of(t, LINKS, 2))
                v.tensor_tensor(yg[:, :], y[:, :], gr[:, :], ALU.mult).then_inc(chain, 1)
                wait(v, chain, of(t, LINKS, 3))
                Xt = X[:, at(t), :].rearrange("p a n -> p (a n)")
                v.tensor_tensor(Xt, Xt, yg[:, :], ALU.add).then_inc(added, 1)

            pipelined(v, NT, [(variance, -1), (take, 1), (norm, -1)])
    sc.close()


def experts(nc, keep, tag, cond, wt, wg, w_gate, w_up, w_down, sw_gate, sw_up, sw_down, load_next):
    sc = Scope(nc, tag)
    sb, ps, sem = sc.sb, sc.ps, sc.sem
    ident, X = keep["ident"], keep["X"]
    SM = 2 * M
    MT = E + SM // M
    CT = 4
    CH = NT // CT
    CW = CT * P
    GD = 64
    RANKED = 1
    hid = sb("hid", [P, MT, CW])
    w_raw = hid[:, :, :].rearrange("p m (n k c) -> p m n k c", n=2, k=KD)
    w_hi = sb("w_hi", [P, MT, 2, KD, M], F32R)
    w_lo = sb("w_lo", [P, MT, 2, KD, M], F32R)
    wdown = sb("wdown", [P, MT, D])
    wtT_in = sb("wtT_in", [E, D])
    wgT_in = sb("wgT_in", [E, GD])
    g_in = sb("g_in", [B, GD])
    wtT = sb("wtT", [P, KD, E])
    wtT_hi = sb("wtT_hi", [P, KD, E], F32R)
    wtT_lo = sb("wtT_lo", [P, KD, E], F32R)
    wgT = sb("wgT", [GD, E])
    gT = sb("gT", [GD, B])
    group_logit = sb("group_logit", [E, B])
    route = sb("route", [P, NT, E])
    top = sb("top", [P, NT, E])
    idx = sb("idx", [P, NT, E], U32)
    idxf = sb("idxf", [P, NT, E])
    lanes_i = sb("lanes_i", [P, E], I32)
    lanes = sb("lanes", [P, E])
    work = sb("work", [P, NT, E])
    z = sb("z", [P, NT])
    s12 = sb("s12", [P, NT, 2])
    sden = sb("sden", [P, NT])
    pick = sb("pick", [P, 2, NT, E])
    xT_hi = sb("xT_hi", [P, KD, NT * P], F32R)
    xT_lo = sb("xT_lo", [P, KD, NT * P], F32R)
    gate_act = sb("gate_act", [P, CH, CW])
    gate_sb, act_sb = gate_act[:, 0:2, :], gate_act[:, 2:4, :]
    logit_T = gate_act[0:E, :, :]
    pg = ps("pg", [P, 2, CW])
    pu = ps("pu", [P, 2, CW])
    py = ps("py", [P, CT, ONE_BANK])
    router_in, weights_in, router_turned, router_taken, grouped, group_taken = (
        sem(n) for n in ("router_in", "weights_in", "router_turned", "router_taken", "grouped", "group_taken"))
    hi_split, lo_split, x_split, wt_hi_made = (sem(n) for n in ("hi_split", "lo_split", "x_split", "wt_hi_made"))
    turned, taken, logit, logit_taken, logit_turned, lanes_made, chain, exp_in, expd, routed = (
        sem(n) for n in ("turned", "taken", "logit", "logit_taken", "logit_turned", "lanes_made", "chain",
                         "exp_in", "expd", "routed"))
    hidden, gate_taken, leaky, up_used, down, summed = (
        sem(n) for n in ("hidden", "gate_taken", "leaky", "up_used", "down", "summed"))

    def in_chunks(eng, before, now):
        for m in range(MT):
            before(0, m)
            now(1, m)
        with eng.Fori(2, CH) as i:
            for m in range(MT):
                before(i - 1, m)
                now(i, m)

    def times(pe, out, pair, k, i):
        cols = slice(i * CW, (i + 1) * CW) if isinstance(i, int) else bass.ds(i * CW, CW)
        hi, lo = pair
        pe.matmul(out, hi, xT_hi[:, k, cols], start=k == 0, stop=False)
        pe.matmul(out, hi, xT_lo[:, k, cols], start=False, stop=False)
        return pe.matmul(out, lo, xT_hi[:, k, cols], start=False, stop=k == KD - 1)

    with nc.Block() as block:
        @block.sync
        def _(sp):
            sp.dma_start(wtT_in[:, :], wt).then_inc(router_in, 16)
            sp.dma_start(wgT_in[:, :], wg).then_inc(router_in, 16)
            sp.dma_start(g_in[:, :], cond).then_inc(router_in, 16)
            for k in range(KD):
                rows = slice(k * P, (k + 1) * P)
                for n, many, shared in ((0, w_gate, sw_gate), (1, w_up, sw_up)):
                    sp.dma_start(w_raw[:, 0:E, n, k, :], many[:, rows, :].rearrange("e p m -> p e m")).then_inc(weights_in, 16)
                    sp.dma_start(w_raw[:, E:MT, n, k, :], shared[rows, :].rearrange("p (e m) -> p e m", m=M)).then_inc(weights_in, 16)
            sp.dma_start(wdown[:, 0:E, :], w_down.rearrange("e p n -> p e n")).then_inc(weights_in, 16)
            sp.dma_start(wdown[:, E:MT, :], sw_down.rearrange("(e p) n -> p e n", p=P)).then_inc(weights_in, 16)
            load_next(sp)

        @block.gpsimd
        def _(pool):
            pool.iota(lanes_i[:, :], [[1, E]], base=0, channel_multiplier=0).then_inc(lanes_made, 1)
            for m in range(MT):
                pool.wait_ge(hi_split, m + 1)
                pool.tensor_tensor(w_lo[:, m, :, :, :], w_raw[:, m, :, :, :], w_hi[:, m, :, :, :].bitcast(F32),
                                   ALU.subtract).then_inc(lo_split, 1)

        def x_bank(t):
            return (pg, pu)[t // 2 % 2][:, t % 2, 0:KD * P]

        @block.tensor
        def _(pe):
            for t in range(NT):
                wait(pe, x_split, t - 3)
                for k in range(KD):
                    last = pe.transpose(x_bank(t)[:, k * P:(k + 1) * P], X[:, t, k * P:(k + 1) * P], ident[:, :])
                last.then_inc(turned, 1)
            pe.wait_ge(router_in, 16 * 3)
            for k in range(KD):
                pe.transpose(py[:, 0, k * E:(k + 1) * E], wtT_in[:, k * P:(k + 1) * P], ident[0:E, 0:E])
            pe.transpose(py[0:GD, 0, 64:64 + E], wgT_in[:, :], ident[0:E, 0:E])
            pe.transpose(py[0:GD, 0, 128:128 + B], g_in[:, :], ident[0:B, 0:B]).then_inc(router_turned, 1)
            pe.wait_ge(router_taken, 1)
            pe.matmul(py[0:E, 1, 0:B], wgT[:, :], gT[:, :], start=True, stop=True).then_inc(grouped, 1)
            pe.wait_ge(x_split, NT)
            pe.wait_ge(group_taken, 1)
            for c in range(CH):
                for k in range(KD):
                    last = times(pe, py[0:E, c, :], (wtT_hi[:, k, :], wtT_lo[:, k, :]), k, c)
                last.then_inc(logit, 1)

            def up(i, m):
                wait(pe, gate_taken, i * MT + (m - 1))
                wait(pe, up_used, i * MT + (m - 1))
                if isinstance(i, int) and i == 0:
                    pe.wait_ge(lo_split, m + 1)
                for n, out in enumerate((pg, pu)):
                    for k in range(KD):
                        last = times(pe, out[:, m % 2, :], (w_hi[:, m, n, k, :], w_lo[:, m, n, k, :]), k, i)
                last.then_inc(hidden, 1)

            def down_from(i, m):
                wait(pe, up_used, i * MT + (m + 1))
                for c in range(CT):
                    wait(pe, summed, i * (MT * CT) + (m * CT + c + 1 - CT))
                    pe.matmul(py[:, c, 0:D], hid[:, m, c * P:(c + 1) * P], wdown[:, m, :], start=True, stop=True).then_inc(down, 1)

            pe.wait_ge(logit_taken, CH)
            for t in range(NT):
                last = pe.transpose(py[:, 0, t * E:(t + 1) * E], logit_T[:, t // CT, t % CT * P:(t % CT + 1) * P], ident[0:E, 0:E])
            last.then_inc(logit_turned, 1)
            for m in range(MT):
                up(0, m)
            pe.wait_ge(weights_in, 16 * (4 * KD + 2))
            pe.wait_ge(routed, 1)
            in_chunks(pe, down_from, up)
            for m in range(MT):
                down_from(CH - 1, m)

        @block.scalar
        def _(a):
            for t in range(NT):
                a.wait_ge(turned, t + 1)
                a.activation(xT_hi[:, :, t * P:(t + 1) * P], x_bank(t).rearrange("p (k n) -> p k n", k=KD),
                             ACT.Copy).then_inc(taken, 1)
            a.wait_ge(weights_in, 16 * (4 * KD + 2))

            def split_weights(m):
                a.activation(w_hi[:, m, :, :, :], w_raw[:, m, :, :, :], ACT.Copy).then_inc(hi_split, 1)

            def gate(i, m):
                wait(a, hidden, i * MT + (m + 1))
                wait(a, leaky, i * MT + (m - 1))
                a.activation(gate_sb[:, m % 2, :], pg[:, m % 2, :], ACT.Copy).then_inc(gate_taken, 1)

            split_weights(0)
            split_weights(1)
            for m in range(MT):
                if m + 2 < MT:
                    split_weights(m + 2)
                gate(0, m)
                if m == RANKED:
                    a.wait_ge(exp_in, 1)
                    a.activation(work[:, :, :], work[:, :, :], ACT.Exp).then_inc(expd, 1)
            with a.Fori(1, CH) as i:
                for m in range(MT):
                    gate(i, m)

        @block.vector
        def _(v):
            done = [0]

            def link(ins):
                done[0] += 1
                ins.then_inc(chain, 1)
                v.wait_ge(chain, done[0])

            def rank():
                v.wait_ge(logit_turned, 1)
                link(v.tensor_copy(route[:, :, :], py[:, 0, 0:NT * E].rearrange("p (t e) -> p t e", e=E)))
                for t in range(NT):
                    last = v.max(top[:, t, :], route[:, t, :])
                link(last)
                for t in range(NT):
                    last = v.max_index(idx[:, t, :], top[:, t, :], route[:, t, :])
                link(last)
                link(v.tensor_copy(idxf[:, :, :], idx[:, :, :]))
                v.tensor_tensor(work[:, :, :], top[:, :, :], spread(top[:, :, 0], E), ALU.subtract).then_inc(exp_in, 1)

            def shares():
                v.wait_ge(expd, 1)
                link(v.tensor_reduce(z[:, :], work[:, :, :], AX_X, ALU.add))
                link(v.reciprocal(z[:, :], z[:, :]))
                link(v.tensor_tensor(s12[:, :, :], work[:, :, 0:2], spread(z[:, :], 2), ALU.mult))
                link(v.tensor_tensor(sden[:, :], s12[:, :, 0], s12[:, :, 1], ALU.add))
                link(v.tensor_scalar(sden[:, :], sden[:, :], 1e-20, None, ALU.add))
                link(v.reciprocal(sden[:, :], sden[:, :]))
                link(v.tensor_tensor(s12[:, :, :], s12[:, :, :], spread(sden[:, :], 2), ALU.mult))

            def weights():
                for n in range(2):
                    link(v.tensor_tensor(pick[:, n, :, :], repeat(lanes[:, :], NT), spread(idxf[:, :, n], E), ALU.is_equal))
                    link(v.tensor_tensor(pick[:, n, :, :], pick[:, n, :, :], spread(s12[:, :, n], E), ALU.mult))
                v.tensor_tensor(route[:, :, :], pick[:, 0, :, :], pick[:, 1, :, :], ALU.add).then_inc(routed, 1)

            def gated(i, m):
                wait(v, gate_taken, i * MT + (m + 1))
                v.scalar_tensor_tensor(out=act_sb[:, m % 2, :], in0=gate_sb[:, m % 2, :], scalar=0.01,
                                       in1=gate_sb[:, m % 2, :], op0=ALU.mult, op1=ALU.max).then_inc(leaky, 1)
                wait(v, leaky, i * MT + (m + 1))
                if not isinstance(i, int) or i > 0:
                    wait(v, down, i * (MT * CT) + ((m + 1 - MT) * CT))
                v.tensor_tensor(hid[:, m, :], act_sb[:, m % 2, :], pu[:, m % 2, :], ALU.mult).then_inc(up_used, 1)

            def add_up(i, m):
                for c in range(CT):
                    tile = slice(i * CT + c, i * CT + c + 1) if isinstance(i, int) else bass.ds(i * CT + c, 1)
                    Xt = X[:, tile, :].rearrange("p a n -> p (a n)")
                    wait(v, down, i * (MT * CT) + (m * CT + c + 1))
                    wait(v, summed, i * (MT * CT) + (m * CT + c + 1 - CT))
                    if m < E:
                        v.scalar_tensor_tensor(out=Xt, in0=py[:, c, 0:D],
                                               scalar=route[:, tile, m:m + 1].rearrange("p a n -> p (a n)"),
                                               in1=Xt, op0=ALU.mult, op1=ALU.add).then_inc(summed, 1)
                    else:
                        v.tensor_tensor(Xt, py[:, c, 0:D], Xt, ALU.add).then_inc(summed, 1)

            for t in range(NT):
                v.wait_ge(taken, t + 1)
                cols = slice(t * P, (t + 1) * P)
                v.tensor_tensor(xT_lo[:, :, cols], x_bank(t).rearrange("p (k n) -> p k n", k=KD),
                                xT_hi[:, :, cols].bitcast(F32), ALU.subtract).then_inc(x_split, 1)
            v.wait_ge(lanes_made, 1)
            v.tensor_copy(lanes[:, :], lanes_i[:, :])
            v.wait_ge(router_turned, 1)
            v.tensor_copy(wtT[:, :, :], py[:, 0, 0:KD * E].rearrange("p (k e) -> p k e", k=KD))
            v.tensor_copy(wtT_hi[:, :, :], py[:, 0, 0:KD * E].rearrange("p (k e) -> p k e", k=KD)).then_inc(wt_hi_made, 1)
            v.wait_ge(wt_hi_made, 1)
            v.tensor_tensor(wtT_lo[:, :, :], wtT[:, :, :], wtT_hi[:, :, :].bitcast(F32), ALU.subtract)
            v.tensor_copy(wgT[:, :], py[0:GD, 0, 64:64 + E])
            v.tensor_copy(gT[:, :], py[0:GD, 0, 128:128 + B]).then_inc(router_taken, 1)
            v.wait_ge(grouped, 1)
            v.tensor_copy(group_logit[:, :], py[0:E, 1, 0:B]).then_inc(group_taken, 1)
            v.wait_ge(group_taken, 1)
            for c in range(CH):
                v.wait_ge(logit, c + 1)
                b = c * CT // RT
                v.tensor_scalar(logit_T[:, c, :], py[0:E, c, :], group_logit[:, b:b + 1], 0.5,
                                ALU.add, ALU.mult).then_inc(logit_taken, 1)
            for m in range(MT):
                gated(0, m)
                if m == RANKED:
                    rank()
                if m == RANKED + 2:
                    shares()
                if m == RANKED + 4:
                    weights()
            v.wait_ge(routed, 1)
            in_chunks(v, add_up, gated)
            for m in range(MT):
                add_up(CH - 1, m)
    sc.close()


def program(nc, t, out):
    with ExitStack() as ctx:
        def sb(name, shape, dt=F32):
            return ctx.enter_context(nc.sbuf_tensor(name, shape, dt))
        keep = {
            "ident": sb("ident", [P, P]), "X": sb("X", [P, NT, D]),
            "K1": sb("K1", [P, B * S], F32R), "K2": sb("K2", [DH + 1, B * S], F32R),
            "V": sb("V", [P, NT, 2 * DH], F16), "v_back": sb("v_back", [P, 1]), "NS": sb("NS", [P, H, NT]), "NV": sb("NV", [P, DH]),
        }
        shifted = [nc.dram_tensor(f"shifted{l}", (H, P + 1, PITCH), F32, kind="Internal").ap() for l in range(2)]
        keep["table"] = [sb(f"table{l}", [H, PITCH]) for l in range(2)]
        stored = [ctx.enter_context(nc.semaphore(f"stored{l}")) for l in range(2)]
        qT_dram = nc.dram_tensor("qT", (H, P, B * S), F32, kind="Internal").ap()
        o_dram = nc.dram_tensor("o", (NT, P, H * DH), F32, kind="Internal").ap()
        x_tiles = t["x"].rearrange("b (t p) d -> p (b t) d", p=P)
        out_tiles = out.rearrange("b (t p) d -> p (b t) d", p=P)

        keep["w"] = {
            "Wq": sb("Wq", [P, KD, H * DH]), "Wkv": sb("Wkv", [P, KD, 2 * DH]), "gcol": sb("gcol", [P, KD]),
            "qsr": sb("qsr", [P, DH]), "ksr": sb("ksr", [P, DH]), "nb": sb("nb", [P, H]),
            "mask8": sb("mask8", [P, NT], U8), "null_key": sb("null_key", [P, DH]),
            "Wout": sb("Wout", [P, H * DH // P, D]), "g_out": sb("g_out", [P, D]),
        }
        proj_in = {L: ctx.enter_context(nc.semaphore(f"proj_in_{L}")) for L in ("L0", "L2", "L3")}
        out_in = {L: ctx.enter_context(nc.semaphore(f"out_in_{L}")) for L in ("L0", "L2", "L3")}
        null_in = ctx.enter_context(nc.semaphore("null_in"))
        keep["null_in"] = null_in

        def arg(L, name):
            return t[f"{L}_cond_{name}"]

        def projection_of(L):
            def loads(sp):
                if L == "L2":
                    load_projection(sp, keep["w"], proj_in[L], arg(L, "g_in"), arg(L, "Wq"), arg(L, "Wkv"),
                                    arg(L, "null_attn_bias"), t["mask_BxS_bk0"])
                else:
                    load_projection(sp, keep["w"], proj_in[L], arg(L, "g_norm"), arg(L, "Wq"), arg(L, "Wkv"),
                                    arg(L, "null_attn_bias"), t["mask_BxS_bf1"], (arg(L, "q_scale"), arg(L, "k_scale")))
            return loads

        def output_of(L):
            def loads(sp):
                load_output(sp, keep["w"], out_in[L], arg(L, "Wo" if L == "L2" else "Wout"), arg(L, "g_out"))
            return loads

        def first_loads(sp):
            projection_of("L0")(sp)
            sp.dma_start(keep["w"]["null_key"][:, :], row_of(t["cond_64"], DH)).then_inc(null_in, 16)
            sp.dma_start(keep["NV"][:, :], row_of(t["cond_64"][1:2, :], DH)).then_inc(null_in, 16)

        def after_experts(sp):
            projection_of("L2")(sp)
            write_table(sp, keep["table"][1], shifted[1], stored[1])

        def none(sp):
            pass

        def attention(L, bias, cosine, load_next, table_stored=None, store_to=None):
            project(nc, keep, f"{L}p", cosine, proj_in[L], qT_dram, table_stored)
            attend(nc, keep, f"{L}a", cosine, bias, qT_dram, o_dram, output_of(L))
            merge(nc, keep, f"{L}m", out_in[L], o_dram, load_next, store_to)

        bias_tables(nc, keep, x_tiles, [[arg(L, n) for n in ("w0", "b0", "g0", "w1", "b1", "g1", "w2", "b2")]
                                        for L in ("L0", "L3")], shifted, stored, first_loads)
        attention("L0", shifted[0], True, none, stored[0])
        experts(nc, keep, "L1", t["cond_64"], *(arg("L1", n) for n in (
            "wt", "wg", "w_gate", "w_up", "w_down", "sw_gate", "sw_up", "sw_down")), after_experts)
        attention("L2", t["fside_16xSxS_0"], False, projection_of("L3"))
        attention("L3", shifted[1], True, none, stored[1], out_tiles)


def kernel(**inputs):
    import concourse.bacc as bacc
    from concourse.bass_utils import run_bass_kernel_spmd

    nc = bacc.Bacc("TRN2", target_bir_lowering=False, num_devices=1)
    arrays, args = {}, {}
    for name, value in inputs.items():
        a = np.ascontiguousarray(value)
        arrays[f"in_{name}"] = a
        args[name] = nc.dram_tensor(f"in_{name}", a.shape, mybir.dt.from_np(a.dtype), kind="ExternalInput").ap()
    out = nc.dram_tensor("out", (B, S, D), F32, kind="ExternalOutput").ap()
    program(nc, args, out)
    r = run_bass_kernel_spmd(nc, [arrays], core_ids=[0])
    return r.results[0]["out"]
```
